# Optimizing a Trainium2 kernel written in Bass

```python
import numpy as np
import jax
import jax.numpy as jnp

def _softmax(x, axis=-1):
    return jax.nn.softmax(x, axis=axis)

def _gelu(x):
    return jax.nn.gelu(x, approximate=True)

def _silu(x):
    return jax.nn.silu(x)

def _sigmoid(x):
    return jax.nn.sigmoid(x)

def _layernorm(x, axis=-1, eps=1e-05):
    m = jnp.mean(x, axis=axis, keepdims=True)
    v = jnp.var(x, axis=axis, keepdims=True)
    return (x - m) / jnp.sqrt(v + eps)

def _scatter_add(tgt, idx, src, axis=0):
    return tgt.at[idx].add(src)

def _segment_sum(src, seg, n):
    return jax.ops.segment_sum(src, seg, n)
kernel_name = 'mk_macaron_d1_jaxref_r4_d70efa'

def setup_inputs(seed: int=0):
    np.random.seed(seed)
    _w = jnp.asarray

    def _L0_attn_setup():
        import jax, jax.numpy as jnp
        import numpy as np
        D_MODEL = 512
        HEAD_SIZE = 64
        N_HEAD = D_MODEL // HEAD_SIZE
        B, T = (2, 256)

        def _layernorm(x, gamma, beta, eps=1e-05):
            mu = jnp.mean(x, axis=-1, keepdims=True)
            var = jnp.var(x, axis=-1, keepdims=True)
            return (x - mu) * jax.lax.rsqrt(var + eps) * gamma + beta

        def _reference_tuple_inner(x, Wx, Ww, bw, Wk, Wv, Wr, Wout, gamma, beta):
            b, t, c = x.shape
            h, n = (N_HEAD, HEAD_SIZE)
            xn = _layernorm(x, gamma, beta)
            w = jax.nn.sigmoid(jnp.einsum('btc,cd->btd', jnp.einsum('btc,cd->btd', xn, Wx), Ww) + bw)
            k = jnp.einsum('btc,cd->btd', xn, Wk)
            v = jnp.einsum('btc,cd->btd', xn, Wv)
            r = jax.nn.sigmoid(jnp.einsum('btc,cd->btd', xn, Wr))

            def tm(a):
                return a.reshape(b, t, h, n).transpose(1, 0, 2, 3)
            k, v, w, r = (tm(k), tm(v), tm(w), tm(r))
            state0 = jnp.zeros((b, h, n, n), x.dtype)

            def step(state, inp):
                k_t, v_t, w_t, r_t = inp
                kv = k_t[..., :, None] * v_t[..., None, :]
                state = (1.0 - w_t)[..., :, None] * state + kv
                y_t = jnp.einsum('bhi,bhij->bhj', r_t, state)
                return (state, y_t)
            state, ys = jax.lax.scan(step, state0, (k, v, w, r))
            y = ys.transpose(1, 0, 2, 3).reshape(b, t, c)
            out = jnp.einsum('btc,cd->btd', y, Wout)
            return (out, state)
        key = jax.random.key(seed)
        ks = jax.random.split(key, 8)
        s = 1.0 / np.sqrt(D_MODEL)
        return {'x': jax.random.normal(ks[0], (B, T, D_MODEL), jnp.float32), 'Wx': jax.random.normal(ks[1], (D_MODEL, D_MODEL), jnp.float32) * s, 'Ww': jax.random.normal(ks[2], (D_MODEL, D_MODEL), jnp.float32) * s, 'bw': jnp.zeros((D_MODEL,), jnp.float32), 'Wk': jax.random.normal(ks[3], (D_MODEL, D_MODEL), jnp.float32) * s, 'Wv': jax.random.normal(ks[4], (D_MODEL, D_MODEL), jnp.float32) * s, 'Wr': jax.random.normal(ks[5], (D_MODEL, D_MODEL), jnp.float32) * s, 'Wout': jax.random.normal(ks[6], (D_MODEL, D_MODEL), jnp.float32) * s, 'gamma': jnp.ones((D_MODEL,), jnp.float32), 'beta': jnp.zeros((D_MODEL,), jnp.float32)}
    _L0_attn_in = _L0_attn_setup()

    def _L0_ffn_setup():
        import jax, jax.numpy as jnp
        import numpy as np
        B, S, D, H = (4, 512, 512, 2048)

        def fwht(x):
            orig_shape = x.shape
            n = orig_shape[-1]
            x = x.reshape(-1, n)
            h = 1
            while h < n:
                xb = x.reshape(-1, n // (2 * h), 2, h)
                a = xb[:, :, 0, :]
                b = xb[:, :, 1, :]
                x = jnp.stack([a + b, a - b], axis=2).reshape(-1, n)
                h *= 2
            scale = jnp.asarray(1.0 / np.sqrt(n), dtype=x.dtype)
            return (x * scale).reshape(orig_shape)
        key = jax.random.key(seed)
        kx, k1, k2, k3 = jax.random.split(key, 4)
        x = jax.random.normal(kx, (B, S, D), dtype=jnp.float32)
        W1 = jax.random.normal(k1, (H, D), dtype=jnp.float32) * (1.0 / np.sqrt(D))
        W2 = jax.random.normal(k2, (D, H), dtype=jnp.float32) * (1.0 / np.sqrt(H))
        W3 = jax.random.normal(k3, (H, D), dtype=jnp.float32) * (1.0 / np.sqrt(D))
        return {'x': x, 'W1': W1, 'W2': W2, 'W3': W3}
    _L0_ffn_in = _L0_ffn_setup()
    _d = {'L0_attn_x': _L0_attn_in['x'], 'L0_attn_Wx': _L0_attn_in['Wx'], 'L0_attn_Ww': _L0_attn_in['Ww'], 'L0_attn_bw': _L0_attn_in['bw'], 'L0_attn_Wk': _L0_attn_in['Wk'], 'L0_attn_Wv': _L0_attn_in['Wv'], 'L0_attn_Wr': _L0_attn_in['Wr'], 'L0_attn_Wout': _L0_attn_in['Wout'], 'L0_attn_gamma': _L0_attn_in['gamma'], 'L0_attn_beta': _L0_attn_in['beta'], 'L0_ffn_W1': _L0_ffn_in['W1'], 'L0_ffn_W2': _L0_ffn_in['W2'], 'L0_ffn_W3': _L0_ffn_in['W3']}
    _x0 = _d['L0_attn_x']
    _d['L0_attn_x'] = jax.random.normal(jax.random.fold_in(jax.random.key(seed), 1), (2, 1024, 512), dtype=_x0.dtype)
    del _x0
    return _d

def reference(L0_attn_x, L0_attn_Wx, L0_attn_Ww, L0_attn_bw, L0_attn_Wk, L0_attn_Wv, L0_attn_Wr, L0_attn_Wout, L0_attn_gamma, L0_attn_beta, L0_ffn_W1, L0_ffn_W2, L0_ffn_W3):

    def _L0_attn_ref(x, Wx, Ww, bw, Wk, Wv, Wr, Wout, gamma, beta):
        import jax, jax.numpy as jnp
        import numpy as np
        D_MODEL = 512
        HEAD_SIZE = 64
        N_HEAD = D_MODEL // HEAD_SIZE
        B, T = (2, 256)

        def _layernorm(x, gamma, beta, eps=1e-05):
            mu = jnp.mean(x, axis=-1, keepdims=True)
            var = jnp.var(x, axis=-1, keepdims=True)
            return (x - mu) * jax.lax.rsqrt(var + eps) * gamma + beta

        def _reference_tuple_inner(x, Wx, Ww, bw, Wk, Wv, Wr, Wout, gamma, beta):
            b, t, c = x.shape
            h, n = (N_HEAD, HEAD_SIZE)
            xn = _layernorm(x, gamma, beta)
            w = jax.nn.sigmoid(jnp.einsum('btc,cd->btd', jnp.einsum('btc,cd->btd', xn, Wx), Ww) + bw)
            k = jnp.einsum('btc,cd->btd', xn, Wk)
            v = jnp.einsum('btc,cd->btd', xn, Wv)
            r = jax.nn.sigmoid(jnp.einsum('btc,cd->btd', xn, Wr))

            def tm(a):
                return a.reshape(b, t, h, n).transpose(1, 0, 2, 3)
            k, v, w, r = (tm(k), tm(v), tm(w), tm(r))
            state0 = jnp.zeros((b, h, n, n), x.dtype)

            def step(state, inp):
                k_t, v_t, w_t, r_t = inp
                kv = k_t[..., :, None] * v_t[..., None, :]
                state = (1.0 - w_t)[..., :, None] * state + kv
                y_t = jnp.einsum('bhi,bhij->bhj', r_t, state)
                return (state, y_t)
            state, ys = jax.lax.scan(step, state0, (k, v, w, r))
            y = ys.transpose(1, 0, 2, 3).reshape(b, t, c)
            out = jnp.einsum('btc,cd->btd', y, Wout)
            return (out, state)
        return _reference_tuple_inner(x, Wx, Ww, bw, Wk, Wv, Wr, Wout, gamma, beta)[0]

    def _L0_ffn_ref(x, W1, W2, W3):
        import jax, jax.numpy as jnp
        import numpy as np
        B, S, D, H = (4, 512, 512, 2048)

        def fwht(x):
            orig_shape = x.shape
            n = orig_shape[-1]
            x = x.reshape(-1, n)
            h = 1
            while h < n:
                xb = x.reshape(-1, n // (2 * h), 2, h)
                a = xb[:, :, 0, :]
                b = xb[:, :, 1, :]
                x = jnp.stack([a + b, a - b], axis=2).reshape(-1, n)
                h *= 2
            scale = jnp.asarray(1.0 / np.sqrt(n), dtype=x.dtype)
            return (x * scale).reshape(orig_shape)
        up_gate = jnp.einsum('bsd,hd->bsh', x, W1)
        up_lin = jnp.einsum('bsd,hd->bsh', x, W3)
        hidden = jax.nn.silu(up_gate) * up_lin
        hidden = fwht(hidden)
        out = jnp.einsum('bsh,dh->bsd', hidden, W2)
        return out
    x = L0_attn_x
    x = x + 0.5 * _L0_ffn_ref(_layernorm(x, axis=-1), L0_ffn_W1, L0_ffn_W2, L0_ffn_W3)
    x = x + _L0_attn_ref(_layernorm(x, axis=-1), L0_attn_Wx, L0_attn_Ww, L0_attn_bw, L0_attn_Wk, L0_attn_Wv, L0_attn_Wr, L0_attn_Wout, L0_attn_gamma, L0_attn_beta)
    x = x + 0.5 * _L0_ffn_ref(_layernorm(x, axis=-1), L0_ffn_W1, L0_ffn_W2, L0_ffn_W3)
    return x

_drawn_inputs = setup_inputs


def setup_inputs(seed=0):
    import zlib

    import numpy as np

    out = dict(_drawn_inputs(seed))
    spreads = {'L0_attn_bw': (0.0, 0.1), 'L0_attn_gamma': (1.0, 0.2), 'L0_attn_beta': (0.0, 0.1)}
    factors = {}
    for name, (base, spread) in spreads.items():
        noise = np.random.default_rng([zlib.crc32(name.encode()), seed]).standard_normal(out[name].shape)
        drawn = base * np.exp(spread * noise) if base else spread * noise
        out[name] = jnp.asarray(drawn.astype(out[name].dtype))
    for name, factor in factors.items():
        out[name] = (out[name] * factor).astype(out[name].dtype)
    return out
```

```python
import concourse.bass as bass
from concourse import mybir
from contextlib import ExitStack

F32 = mybir.dt.float32
F32R = mybir.dt.float32r
I32 = mybir.dt.int32
ALU = mybir.AluOpType
ACT = mybir.ActivationFunctionType

P = 128
B, T, D, H = 2, 1024, 512, 2048
NT = B * T // P
KD = D // P
TC = 512
NC = B * T // TC
TPC = TC // P
GH = 256
NG = H // GH
HT = GH // P
EPS = 1e-5
HS = 64
NPAIR = D // P
LEVELS = [1, 2, 4, 8, 16, 32, 64]
MAGIC = 0x5F3759DF


def rsqrt_newton(nc, dve, step, count, v, y, t):
    def then(op):
        op.then_inc(step, 1)
        dve.wait_ge(step, count())
    then(nc.vector.tensor_scalar(t.bitcast(I32), v.bitcast(I32), 1, None, ALU.logical_shift_right))
    then(nc.vector.tensor_scalar(y.bitcast(I32), t.bitcast(I32), -1.0, float(MAGIC), ALU.mult, ALU.add))
    for _ in range(4):
        then(nc.vector.tensor_tensor(t, y, y, ALU.mult))
        then(nc.vector.tensor_tensor(t, t, v, ALU.mult))
        then(nc.vector.tensor_scalar(t, t, -0.5, 1.5, ALU.mult, ALU.add))
        then(nc.vector.tensor_tensor(y, y, t, ALU.mult))


def prepare_weights(nc, w2t, wxt, attn_w, had, w2p, attn_hi, attn_lo):
    NB = H // P
    with ExitStack() as ctx:
        def sb(name, shape, dt=F32):
            return ctx.enter_context(nc.sbuf_tensor(name, shape, dt))

        def sem(name):
            return ctx.enter_context(nc.semaphore(name))
        fly = [sb(f"fly{i}", [P, NB, D]) for i in range(2)]
        hmat = sb("hmat", [P, P])
        wx_sb = sb("wx_sb", [P, KD, D])
        raw = sb("raw_attn", [P, 5, KD, D])
        part_hi = sb("part_hi", [P, 2, KD, D], F32R)
        part_lo = sb("part_lo", [P, 2, KD, D], F32R)
        w2o = sb("w2o", [P, 4, D])
        ps = [ctx.enter_context(nc.psum_tensor(f"prep_ps{i}", [P, D], F32)) for i in range(4)]
        w2_loaded = sem("w2_loaded")
        had_loaded = sem("had_loaded")
        wx_loaded = sem("wx_loaded")
        raw_loaded = sem("raw_loaded")
        fly_v = sem("fly_v")
        fly_p = sem("fly_p")
        prod = sem("prod")
        out_copied = sem("out_copied")
        w2_stored = [sem(f"w2_stored{i}") for i in range(4)]
        hi_split = sem("hi_split")
        lo_split = sem("lo_split")
        split_stored = [sem(f"split_stored{i}") for i in range(2)]
        block = ctx.enter_context(nc.Block())
        HALF = 320
        STAGES = 4

        @block.sync
        def _(sp):
            sp.dma_start(fly[0][:, :, :], w2t.rearrange("(b p) d -> p b d", p=P)).then_inc(w2_loaded, 16)
            sp.dma_start(hmat[:, :], had).then_inc(had_loaded, 16)
            sp.dma_start(wx_sb[:, :, :], wxt.rearrange("(k p) d -> p k d", p=P)).then_inc(wx_loaded, 16)
            for n in range(5):
                sp.dma_start(raw[:, n, :, :], attn_w[n].rearrange("(k p) d -> p k d", p=P)).then_inc(raw_loaded, 16)
            for n in range(5):
                order = [1, 2, 3, 4, 0][n]
                sp.wait_ge(lo_split, n + 1)
                sp.dma_start(attn_hi[order], part_hi[:, n % 2, :, :].bitcast(F32)).then_inc(split_stored[n % 2], 16)
                sp.dma_start(attn_lo[order], part_lo[:, n % 2, :, :].bitcast(F32)).then_inc(split_stored[n % 2], 16)
            for b in range(NB):
                sp.wait_ge(out_copied, KD + b + 1)
                sp.dma_start(w2p[b // HT, :, b % HT, :], w2o[:, b % 4, :]).then_inc(w2_stored[b % 4], 16)
            for i in range(4):
                sp.wait_ge(w2_stored[i], 16 * NB // 4)
            sp.wait_ge(split_stored[0], 32 * 3)
            sp.wait_ge(split_stored[1], 32 * 2)

        def butterfly(eng, engine, s, cols, done):
            h = 1 << s
            src = fly[s % 2][:, :, cols].rearrange("p (n two h) d -> p n two h d", two=2, h=h)
            dst = fly[(s + 1) % 2][:, :, cols].rearrange("p (n two h) d -> p n two h d", two=2, h=h)
            if s:
                eng.wait_ge(done, 2 * s)
            engine.tensor_tensor(dst[:, :, 0], src[:, :, 0], src[:, :, 1], ALU.add).then_inc(done, 1)
            engine.tensor_tensor(dst[:, :, 1], src[:, :, 0], src[:, :, 1], ALU.subtract).then_inc(done, 1)

        @block.vector
        def _(dve):
            dve.wait_ge(w2_loaded, 16)
            for s in range(STAGES):
                butterfly(dve, nc.vector, s, slice(0, HALF), fly_v)

        @block.gpsimd
        def _(pool):
            pool.wait_ge(w2_loaded, 16)
            for s in range(STAGES):
                butterfly(pool, nc.gpsimd, s, slice(HALF, D), fly_p)
            for n in range(5):
                pool.wait_ge(hi_split, n + 1)
                if n >= 2:
                    pool.wait_ge(split_stored[n % 2], 32 * (n // 2))
                order = [1, 2, 3, 4, 0][n]
                nc.gpsimd.tensor_tensor(part_lo[:, n % 2, :, :], raw[:, order, :, :], part_hi[:, n % 2, :, :],
                                        ALU.subtract).then_inc(lo_split, 1)

        @block.tensor
        def _(pe):
            pe.wait_ge(wx_loaded, 16)
            pe.wait_ge(raw_loaded, 80)
            for m in range(KD):
                for k in range(KD):
                    last = nc.tensor.matmul(ps[m][:, :], wx_sb[:, k, m * P:(m + 1) * P], raw[:, 0, k, :],
                                            start=(k == 0), stop=(k == KD - 1))
                last.then_inc(prod, 1)
            pe.wait_ge(had_loaded, 16)
            pe.wait_ge(fly_v, 2 * STAGES)
            pe.wait_ge(fly_p, 2 * STAGES)
            for b in range(NB):
                pe.wait_ge(out_copied, b + 1)
                nc.tensor.matmul(ps[b % 4][:, :], hmat[:, :], fly[STAGES % 2][:, b, :],
                                 start=True, stop=True).then_inc(prod, 1)

        @block.scalar
        def _(act):
            act.wait_ge(raw_loaded, 80)
            for n in range(4):
                if n >= 2:
                    act.wait_ge(split_stored[n % 2], 32 * (n // 2))
                nc.scalar.activation(part_hi[:, n % 2, :, :], raw[:, n + 1, :, :], ACT.Copy).then_inc(hi_split, 1)
            for m in range(KD):
                act.wait_ge(prod, KD)
                act.wait_ge(prod, m + 1)
                nc.scalar.activation(raw[:, 0, m, :], ps[m][:, :], ACT.Copy).then_inc(out_copied, 1)
            act.wait_ge(out_copied, KD)
            act.wait_ge(split_stored[0], 32 * 2)
            nc.scalar.activation(part_hi[:, 0, :, :], raw[:, 0, :, :], ACT.Copy).then_inc(hi_split, 1)
            for b in range(NB):
                act.wait_ge(prod, KD + b + 1)
                if b >= 4:
                    act.wait_ge(w2_stored[b % 4], 16 * (b // 4))
                nc.scalar.activation(w2o[:, b % 4, :], ps[b % 4][:, :], ACT.Copy,
                                     scale=0.5 / H ** 0.5).then_inc(out_copied, 1)


def feed_forward(nc, tag, x_in, x_out, w1g, w3g, w2p, ident_in):
    with ExitStack() as ctx:
        def sb(name, shape, dt=F32):
            return ctx.enter_context(nc.sbuf_tensor(f"{tag}_{name}", shape, dt))

        def sem(name):
            return ctx.enter_context(nc.semaphore(f"{tag}_{name}"))
        x = sb("x", [P, NT, D])
        xt_hi = sb("xt_hi", [P, KD, NC * TC], F32R)
        xt_lo = sb("xt_lo", [P, KD, NC * TC], F32R)
        raw1 = sb("raw1", [P, 2, KD, GH])
        raw3 = sb("raw3", [P, 2, KD, GH])
        raw2 = sb("raw2", [P, 2, HT, D])
        w1_hi = sb("w1_hi", [P, 2, KD, GH], F32R)
        w1_lo = sb("w1_lo", [P, 2, KD, GH], F32R)
        w3_hi = sb("w3_hi", [P, 2, KD, GH], F32R)
        w3_lo = sb("w3_lo", [P, 2, KD, GH], F32R)
        w2_hi = sb("w2_hi", [P, 2, HT, D], F32R)
        w2_lo = sb("w2_lo", [P, 2, HT, D], F32R)
        silu = sb("silu", [P, 2, TC])
        hid = sb("hid", [P, 2, TC])
        hid_hi = sb("hid_hi", [P, 2, HT, TC], F32R)
        hid_lo = sb("hid_lo", [P, 2, HT, TC], F32R)
        xn = sb("xn", [P, 2, D])
        stats = sb("stats", [P, TPC, 6])
        mv = sb("mv", [P, TPC, 2])
        var = sb("var", [P, TPC])
        rstd = sb("rstd", [P, TPC])
        tmp = sb("tmp", [P, TPC])
        ident = sb("ident", [P, P])

        def bank(name):
            return ctx.enter_context(nc.psum_tensor(f"{tag}_{name}", [P, TC], F32))
        gate = [bank(f"gate{i}") for i in range(HT)]
        lin = [bank(f"lin{i}") for i in range(HT)]
        down = [bank(f"down{i}") for i in range(TPC)]

        ident_loaded = sem("ident_loaded")
        x_loaded = [sem(f"x_loaded{c}") for c in range(NC)]
        raw_loaded = [sem(f"raw_loaded{b}") for b in range(2)]
        waited = sem("waited")
        weights_hi = sem("weights_hi")
        weights_lo = sem("weights_lo")
        ln_step = sem("ln_step")
        xn_ready = sem("xn_ready")
        transposed = sem("transposed")
        xt_hi_ready = sem("xt_hi_ready")
        xt_ready = sem("xt_ready")
        gate_done = sem("gate_done")
        lin_done = sem("lin_done")
        silu_done = sem("silu_done")
        hid_done = sem("hid_done")
        hi_done = sem("hi_done")
        lo_done = sem("lo_done")
        down_done = sem("down_done")
        added = sem("added")
        stored = sem("stored")
        block = ctx.enter_context(nc.Block())
        STEPS = NG * NC
        PER = 2 * NC

        xin_v = x_in.rearrange("(n p) d -> p n d", p=P)
        xout_v = x_out.rearrange("(n p) d -> p n d", p=P)

        @block.sync
        def _(sp):
            sp.dma_start(ident[:, :], ident_in).then_inc(ident_loaded, 16)

            def load_group(g, b):
                sp.dma_start(raw1[:, b, :, :], w1g[g]).then_inc(raw_loaded[b], 16)
                sp.dma_start(raw3[:, b, :, :], w3g[g]).then_inc(raw_loaded[b], 16)
                sp.dma_start(raw2[:, b, :, :], w2p[g]).then_inc(raw_loaded[b], 16)
            for c in range(NC):
                sp.dma_start(x[:, c * TPC:(c + 1) * TPC, :],
                             xin_v[:, c * TPC:(c + 1) * TPC, :]).then_inc(x_loaded[c], 16)
                if c < 2:
                    load_group(c, c)
            with sp.Fori(1, NG // 2) as i:
                for b in range(2):
                    sp.wait_ge(weights_lo, 6 * i + 3 * b - 3)
                    load_group(2 * i + b, b)
            for t in range(NT):
                sp.wait_ge(added, (STEPS - NC) * TPC + t + 1)
                sp.dma_start(xout_v[:, t, :], x[:, t, :]).then_inc(stored, 16)
            sp.wait_ge(stored, 16 * NT)

        @block.gpsimd
        def _(pool):
            def split_group(g3, b, loads, free):
                pool.wait_ge(raw_loaded[b], loads)
                if free is not None:
                    pool.wait_ge(down_done, free)
                pool.sem_inc(waited, 1)
                for raw, hi in ((raw1, w1_hi), (raw3, w3_hi), (raw2, w2_hi)):
                    nc.gpsimd.tensor_copy(hi[:, b], raw[:, b]).then_inc(weights_hi, 1)
                for n, (raw, hi, lo) in enumerate(((raw1, w1_hi, w1_lo), (raw3, w3_hi, w3_lo), (raw2, w2_hi, w2_lo))):
                    pool.wait_ge(weights_hi, g3 + n + 1)
                    nc.gpsimd.tensor_tensor(lo[:, b], raw[:, b], hi[:, b], ALU.subtract).then_inc(weights_lo, 1)
            for b in range(2):
                split_group(3 * b, b, 48, None)
            with pool.Fori(1, NG // 2) as i:
                for b in range(2):
                    split_group(6 * i + 3 * b, b, 48 * i + 48, (2 * i + b - 1) * NC * TPC)

        @block.tensor
        def _(pe):
            def transposes(c, free):
                for j in range(TPC):
                    t = c * TPC + j
                    pe.wait_ge(xn_ready, t + 1)
                    free(j)
                    for k in range(KD):
                        last = nc.tensor.transpose(down[j][:, k * P:(k + 1) * P], xn[:, t % 2, k * P:(k + 1) * P], ident[:, :])
                    last.then_inc(transposed, 1)

            def up(n, j, first):
                b, c = (j // NC) % 2, j % NC
                if c == 0:
                    pe.wait_ge(weights_lo, (3 * n) // NC + 3 if isinstance(n, int) else 6 * first + 3 * b + 3)
                for h in range(HT):
                    cols = slice(h * P, (h + 1) * P)
                    for psum, hi, lo, done, used in ((gate[h], w1_hi, w1_lo, gate_done, silu_done),
                                                     (lin[h], w3_hi, w3_lo, lin_done, hid_done)):
                        if not (isinstance(n, int) and n == 0):
                            pe.wait_ge(used, HT * n + h - 1)
                        for k in range(KD):
                            xs = slice(c * TC, (c + 1) * TC)
                            nc.tensor.matmul(psum[:, :], hi[:, b, k, cols], xt_hi[:, k, xs], start=(k == 0), stop=False)
                            nc.tensor.matmul(psum[:, :], hi[:, b, k, cols], xt_lo[:, k, xs], start=False, stop=False)
                            last = nc.tensor.matmul(psum[:, :], lo[:, b, k, cols], xt_hi[:, k, xs],
                                                    start=False, stop=(k == KD - 1))
                        last.then_inc(done, 1)

            def downs(n, j, free):
                b, s = (j // NC) % 2, j % 2
                pe.wait_ge(lo_done, HT * n + HT)
                for t in range(TPC):
                    free(t)
                    cols = slice(t * P, (t + 1) * P)
                    for h in range(HT):
                        nc.tensor.matmul(down[t][:, :], hid_hi[:, s, h, cols], w2_hi[:, b, h, :], start=(h == 0), stop=False)
                        nc.tensor.matmul(down[t][:, :], hid_hi[:, s, h, cols], w2_lo[:, b, h, :], start=False, stop=False)
                        last = nc.tensor.matmul(down[t][:, :], hid_lo[:, s, h, cols], w2_hi[:, b, h, :],
                                                start=False, stop=(h == HT - 1))
                    last.then_inc(down_done, 1)

            def banks_added(n):
                return lambda t: pe.wait_ge(added, TPC * n - TPC + t + 1)

            pe.wait_ge(ident_loaded, 16)
            transposes(0, lambda j: None)
            transposes(1, lambda j: pe.wait_ge(xt_ready, j + 1))
            for n in range(PER):
                if n < NC:
                    pe.wait_ge(xt_ready, TPC * (n + 1))
                up(n, n, 0)
                if n == 0:
                    transposes(2, lambda j: pe.wait_ge(xt_ready, TPC + j + 1))
                if n == 1:
                    downs(0, 0, lambda t: pe.wait_ge(xt_ready, 2 * TPC + t + 1))
                    transposes(3, lambda j: pe.wait_ge(added, j + 1))
                if n == 2:
                    downs(1, 1, lambda t: pe.wait_ge(xt_ready, 3 * TPC + t + 1))
                if n >= 3:
                    downs(n - 1, n - 1, banks_added(n - 1))
            with pe.Fori(1, NG // 2) as i:
                for j in range(PER):
                    up(PER * i + j, j, i)
                    downs(PER * i + (j - 1), (j - 1) % PER, banks_added(PER * i + (j - 1)))
            downs(STEPS - 1, PER - 1, banks_added(STEPS - 1))

        @block.scalar
        def _(act):
            def transposed_hi(c):
                for j in range(TPC):
                    t = c * TPC + j
                    act.wait_ge(transposed, t + 1)
                    nc.scalar.activation(xt_hi[:, :, t * P:(t + 1) * P],
                                         down[j][:, :].rearrange("p (k t) -> p k t", k=KD), ACT.Copy).then_inc(xt_hi_ready, 1)

            def hidden(n, j):
                for h in range(HT):
                    start = isinstance(n, int) and n == 0
                    act.wait_ge(gate_done, HT * n + h + 1)
                    if not start:
                        act.wait_ge(hid_done, HT * n + h - 1)
                    nc.scalar.activation(silu[:, h, :], gate[h][:, :], ACT.Silu).then_inc(silu_done, 1)
                    act.wait_ge(hid_done, HT * n + h + 1)
                    if not (isinstance(n, int) and n < 2):
                        act.wait_ge(down_done, TPC * n - TPC)
                    nc.scalar.activation(hid_hi[:, j % 2, h, :], hid[:, h, :], ACT.Copy).then_inc(hi_done, 1)
            transposed_hi(0)
            transposed_hi(1)
            for n in range(PER):
                hidden(n, n)
                if n == 0:
                    transposed_hi(2)
                if n == 1:
                    transposed_hi(3)
            with act.Fori(1, NG // 2) as i:
                for j in range(PER):
                    hidden(PER * i + j, j)

        @block.vector
        def _(dve):
            steps = [0]

            def count():
                steps[0] += 1
                return steps[0]

            def then(op):
                op.then_inc(ln_step, 1)
                dve.wait_ge(ln_step, count())

            def layernorm(c):
                dve.wait_ge(x_loaded[c], 16)
                for j in range(TPC):
                    op = nc.vector.bn_stats(stats[:, j, :], x[:, c * TPC + j, :])
                    op.then_inc(ln_step, 1)
                    count()
                dve.wait_ge(ln_step, steps[0])
                for j in range(TPC):
                    op = nc.vector.bn_aggr(mv[:, j, :], stats[:, j, :])
                    op.then_inc(ln_step, 1)
                    count()
                dve.wait_ge(ln_step, steps[0])
                then(nc.vector.tensor_scalar(var[:, :], mv[:, :, 1], EPS, None, ALU.add))
                rsqrt_newton(nc, dve, ln_step, count, var[:, :], rstd[:, :], tmp[:, :])
                for j in range(TPC):
                    t = c * TPC + j
                    if t >= 2:
                        dve.wait_ge(transposed, t - 1)
                    nc.vector.tensor_scalar(xn[:, t % 2, :], x[:, t, :], mv[:, j, 0:1], rstd[:, j:j + 1],
                                            ALU.subtract, ALU.mult).then_inc(xn_ready, 1)
                    if j:
                        transposed_lo(t - 1)
                transposed_lo(c * TPC + TPC - 1)

            def transposed_lo(t):
                dve.wait_ge(xt_hi_ready, t + 1)
                cols = slice(t * P, (t + 1) * P)
                nc.vector.tensor_tensor(xt_lo[:, :, cols], down[t % TPC][:, :].rearrange("p (k t) -> p k t", k=KD),
                                        xt_hi[:, :, cols], ALU.subtract).then_inc(xt_ready, 1)

            def hidden(n, j):
                for h in range(HT):
                    start = isinstance(n, int) and n == 0
                    dve.wait_ge(silu_done, HT * n + h + 1)
                    dve.wait_ge(lin_done, HT * n + h + 1)
                    if not start:
                        dve.wait_ge(lo_done, HT * n + h - 1)
                    nc.vector.tensor_tensor(hid[:, h, :], silu[:, h, :], lin[h][:, :], ALU.mult).then_inc(hid_done, 1)
                    dve.wait_ge(hi_done, HT * n + h + 1)
                    nc.vector.tensor_tensor(hid_lo[:, j % 2, h, :], hid[:, h, :], hid_hi[:, j % 2, h, :],
                                            ALU.subtract).then_inc(lo_done, 1)

            def add(n, j, before):
                c = j % NC
                for t in range(TPC):
                    dve.wait_ge(down_done, TPC * n + t + 1)
                    if before:
                        dve.wait_ge(added, TPC * n - NC * TPC + t + 1)
                    xt = x[:, c * TPC + t, :]
                    nc.vector.tensor_tensor(xt, xt, down[t][:, :], ALU.add).then_inc(added, 1)
            layernorm(0)
            layernorm(1)
            for n in range(PER):
                hidden(n, n)
                if n >= 1:
                    add(n - 1, n - 1, n - 1 >= NC)
                if n < 2:
                    layernorm(n + 2)
            with dve.Fori(1, NG // 2) as i:
                for j in range(PER):
                    hidden(PER * i + j, j)
                    add(PER * i + (j - 1), (j - 1) % PER, True)
            add(STEPS - 1, PER - 1, True)


def mixing(nc, x_in, x_out, attn_hi, attn_lo, gamma_in, beta_in, bw_in, ident_in, masks_in):
    CPB = T // TC
    U = CPB * NPAIR
    Q = TC // P
    L = 2 + len(LEVELS)
    UPD = 1 + len(LEVELS)
    TT = CPB * TPC
    LN = CPB * (2 * TPC + 1 + 18 + 3 + 18 + 1)
    ST = NPAIR * 2 * Q + NPAIR * 2 * (Q - 1)
    OFF = [2 * TC - (2 * TC >> i) for i in range(len(LEVELS) + 1)]
    T_AT = {(1, 2): 0, (1, 5): 1, (2, 2): 2, (2, 5): 3}
    V_AT = {(4, 7): 0, (4, 8): 1, (5, 0): 2, (5, 1): 3}
    O_AT = {(5, 2): 0, (5, 3): 1, (5, 4): 2, (5, 5): 3}

    with ExitStack() as ctx:
        def sb(name, shape, dt=F32):
            return ctx.enter_context(nc.sbuf_tensor(f"mix_{name}", shape, dt))

        def sem(name):
            return ctx.enter_context(nc.semaphore(f"mix_{name}"))
        w_hi = [sb(f"{n}_hi", [P, KD, D], F32R) for n in ("wxw", "wk", "wv", "wr", "wo")]
        w_lo = [sb(f"{n}_lo", [P, KD, D], F32R) for n in ("wxw", "wk", "wv", "wr", "wo")]
        WXW, WK, WV, WR, WO = range(5)
        x = sb("x", [P, CPB, TPC, D])
        xn = sb("xn", [P, 2, D])
        z = sb("z", [P, 2, D])
        zt_hi = sb("zt_hi", [P, CPB, KD, TC], F32R)
        zt_lo = sb("zt_lo", [P, CPB, KD, TC], F32R)
        v = sb("v", [P, TPC, D])
        r = sb("r", [P, 2, 2, TC])
        k = sb("k", [P, 2, TC])
        decay = sb("decay", [P, 2, 2 * TC])
        rsum = sb("rsum", [P, TC])
        mt = sb("mt", [P, 2, 2 * Q, P])
        ktok = sb("ktok", [P, TC])
        state = sb("state", [P, 2, Q - 1, P])
        carry = sb("carry", [P, NPAIR, P])
        yt_hi = sb("yt_hi", [P, NPAIR, TC], F32R)
        yt_lo = sb("yt_lo", [P, NPAIR, TC], F32R)
        masks = sb("masks", [P, 1 + len(LEVELS), P], I32)
        ident = sb("ident", [P, P])
        gamma = sb("gamma", [P, KD])
        beta = sb("beta", [P, KD])
        bw = sb("bw", [P, KD])
        neg_bw = sb("neg_bw", [P, KD])
        stats = sb("stats", [P, TPC, 6])
        mv = sb("mv", [P, TPC, 2])
        var = sb("var", [P, TPC])
        rstd = sb("rstd", [P, TPC])
        rstd2 = sb("rstd2", [P, TPC])
        var2 = sb("var2", [P, TPC])
        tmp = sb("tmp", [P, TPC])

        def bank(name):
            return ctx.enter_context(nc.psum_tensor(f"mix_{name}", [P, TC], F32))
        row = [bank(f"row{i}") for i in range(2)]
        pj = [bank(f"pj{i}") for i in range(2)]
        lv = [bank(f"lv{i}") for i in range(2)]
        yb = bank("yb")
        ks = bank("ks")

        consts_loaded = sem("consts_loaded")
        weights_loaded = sem("weights_loaded")
        x_loaded = [sem(f"x_loaded{c}") for c in range(CPB)]
        x_stored = [sem(f"x_stored{c}") for c in range(CPB)]
        cleared = sem("cleared")
        negated = sem("negated")
        waited = sem("waited")
        ln_step = sem("ln_step")
        xn_ready = sem("xn_ready")
        transposed = sem("transposed")
        z_ready = sem("z_ready")
        zhi_ready = sem("zhi_ready")
        zt_ready = sem("zt_ready")
        v_done = sem("v_done")
        v_ready = sem("v_ready")
        proj_done = sem("proj_done")
        proj_used = sem("proj_used")
        lv_done = sem("lv_done")
        lv_used = sem("lv_used")
        updated = sem("updated")
        rsum_ready = sem("rsum_ready")
        kt_done = sem("kt_done")
        ktok_ready = sem("ktok_ready")
        kv_done = sem("kv_done")
        state_step = sem("state_step")
        y_done = sem("y_done")
        yhi_ready = sem("yhi_ready")
        yt_ready = sem("yt_ready")
        out_done = sem("out_done")
        res_done = sem("res_done")
        block = ctx.enter_context(nc.Block())

        xin_v = x_in.rearrange("(b c n p) d -> b c p n d", b=B, c=CPB, p=P)
        xout_v = x_out.rearrange("(b c n p) d -> b c n p d", b=B, c=CPB, p=P)

        def states_before(u, q):
            return (2 * Q * u if u < NPAIR else 2 * Q * NPAIR + 2 * (Q - 1) * (u - NPAIR)) + 2 * q

        @block.sync
        def _(sp):
            for dst, src in ((ident[:, :], ident_in), (masks[:, :, :], masks_in), (gamma[:, :], gamma_in),
                             (beta[:, :], beta_in), (bw[:, :], bw_in)):
                sp.dma_start(dst, src).then_inc(consts_loaded, 16)
            sp.dma_start(x[:, 0, :, :], xin_v[0, 0]).then_inc(x_loaded[0], 16)
            for n in (WV, WR, WK, WXW, WO):
                sp.dma_start(w_hi[n][:, :, :].bitcast(F32), attn_hi[n]).then_inc(weights_loaded, 16)
                sp.dma_start(w_lo[n][:, :, :].bitcast(F32), attn_lo[n]).then_inc(weights_loaded, 16)
            sp.dma_start(x[:, 1, :, :], xin_v[0, 1]).then_inc(x_loaded[1], 16)
            for b in range(B):
                for c in range(CPB):
                    for j in range(TPC):
                        sp.wait_ge(res_done, TT * b + c * TPC + j + 1)
                        sp.dma_start(xout_v[b, c, j], x[:, c, j, :]).then_inc(x_stored[c], 16)
                if b + 1 < B:
                    for c in range(CPB):
                        sp.wait_ge(x_stored[c], 16 * TPC * b + 16 * TPC)
                        sp.dma_start(x[:, c, :, :], xin_v[b + 1, c]).then_inc(x_loaded[c], 16)
            for c in range(CPB):
                sp.wait_ge(x_stored[c], 16 * TPC * B)

        @block.gpsimd
        def _(pool):
            for t in (r[:, :, :, :], mt[:, :, :, :], state[:, :, :, :], carry[:, :, :]):
                nc.gpsimd.memset(t, 0.0).then_inc(cleared, 1)

        @block.tensor
        def _(pe):
            def three(psum, lhs_hi, lhs_lo, rhs_hi, rhs_lo, start, stop):
                nc.tensor.matmul(psum, lhs_hi, rhs_hi, start=start, stop=False)
                nc.tensor.matmul(psum, lhs_hi, rhs_lo, start=False, stop=False)
                return nc.tensor.matmul(psum, lhs_lo, rhs_hi, start=False, stop=stop)

            def transposes(b, c, j):
                pe.wait_ge(xn_ready, TT * b + TPC * c + j + 1)
                if j >= 2:
                    pe.wait_ge(z_ready, TT * b + TPC * c + j - 1)
                elif c:
                    pe.wait_ge(v_ready, TT * b + j + 3)
                t = TPC * c + j
                for kk in range(KD):
                    cols = slice(kk * P, (kk + 1) * P)
                    last = nc.tensor.transpose(row[j % 2][:, cols], xn[:, t % 2, cols], ident[:, :])
                last.then_inc(transposed, 1)

            def v_proj(b, c, j):
                pe.wait_ge(zt_ready, TT * b + TPC * c + j + 1)
                if j >= 2:
                    pe.wait_ge(v_ready, TT * b + TPC * c + j - 1)
                else:
                    pe.wait_ge(z_ready, TT * b + TPC * c + j + 3)
                cols = slice(j * P, (j + 1) * P)
                for kk in range(KD):
                    last = three(row[j % 2][:, :], zt_hi[:, c, kk, cols], zt_lo[:, c, kk, cols],
                                 w_hi[WV][:, kk, :], w_lo[WV][:, kk, :], kk == 0, kk == KD - 1)
                last.then_inc(v_done, 1)

            def out_proj(b, c, j):
                pe.wait_ge(yt_ready, U * b + NPAIR * (c + 1))
                if j >= 2:
                    pe.wait_ge(res_done, TT * b + TPC * c + j - 1)
                elif c:
                    pe.wait_ge(res_done, TT * b + j + 3)
                else:
                    pe.wait_ge(v_ready, TT * b + TPC + j + 3)
                cols = slice(j * P, (j + 1) * P)
                for kk in range(NPAIR):
                    last = three(row[j % 2][:, :], yt_hi[:, kk, cols], yt_lo[:, kk, cols],
                                 w_hi[WO][:, kk, :], w_lo[WO][:, kk, :], kk == 0, kk == NPAIR - 1)
                last.then_inc(out_done, 1)

            def project(b, u, part):
                c, p, job, third = u // NPAIR, u % NPAIR, part // 3, part % 3
                n = 3 * u + job
                if third == 0:
                    pe.wait_ge(zt_ready, TT * b + TPC * (c + 1))
                    if n >= 2:
                        pe.wait_ge(proj_used, 3 * U * b + n - 1)
                w = (WR, WK, WXW)[job]
                cols = slice(p * P, (p + 1) * P)
                passes = [(a, e, kk) for kk in range(KD) for a, e in ((w_hi, zt_hi), (w_hi, zt_lo), (w_lo, zt_hi))]
                for i in range(4 * third, 4 * third + 4):
                    a, e, kk = passes[i]
                    last = nc.tensor.matmul(pj[n % 2][:, :], a[w][:, kk, cols], e[:, c, kk, :],
                                            start=(i == 0), stop=(i == len(passes) - 1))
                if third == 2:
                    last.then_inc(proj_done, 1)

            def level(b, u, l):
                n, ub = L * u + l, u % 2
                if n >= 2:
                    pe.wait_ge(lv_used, L * U * b + n - 1)
                if l == 0:
                    pe.wait_ge(proj_used, 3 * U * b + 3 * u + 2)
                if l >= 2:
                    pe.wait_ge(updated, UPD * U * b + UPD * u + l - 1)
                for i in range(2 if l < 2 else Q):
                    q = 2 * l + i if l < 2 else i
                    cols = slice(q * P, (q + 1) * P)
                    if l < 2:
                        rhs = r[:, ub, :, cols]
                        out = lv[n % 2][:, i * 2 * P:(i + 1) * 2 * P]
                    else:
                        m = LEVELS[l - 2]
                        rhs = r[:, ub, :, cols].rearrange("p h (n two m) -> p h n two m", two=2, m=m)[:, :, :, 1, :]
                        out = lv[n % 2][:, i * P:(i + 1) * P]
                    last = nc.tensor.matmul(out, k[:, ub, cols], rhs, start=True, stop=True)
                last.then_inc(lv_done, 1)

            def k_transposes(b, u):
                pe.wait_ge(updated, UPD * U * b + UPD * (u + 1))
                if u:
                    pe.wait_ge(state_step, ST * b + states_before(u, 0))
                for q in range(Q):
                    cols = slice(q * P, (q + 1) * P)
                    last = nc.tensor.transpose(ks[:, cols], k[:, u % 2, cols], ident[:, :])
                last.then_inc(kt_done, 1)

            def k_times_v(b, u):
                p = u % NPAIR
                pe.wait_ge(ktok_ready, U * b + u + 1)
                pe.wait_ge(v_ready, TT * b + TPC * (u // NPAIR + 1))
                for q in range(Q):
                    cols = slice(q * P, (q + 1) * P)
                    last = nc.tensor.matmul(ks[:, cols], ktok[:, cols], v[:, q, p * P:(p + 1) * P], start=True, stop=True)
                last.then_inc(kv_done, 1)

            def outputs(b, u):
                c, p, ub = u // NPAIR, u % NPAIR, u % 2
                pe.wait_ge(lv_used, L * U * b + L * (u + 1))
                pe.wait_ge(rsum_ready, U * b + u + 1)
                pe.wait_ge(state_step, ST * b + states_before(u, Q - 1))
                if u:
                    pe.wait_ge(yt_ready, U * b + u)
                for q in range(Q):
                    cols = slice(q * P, (q + 1) * P)
                    has_state = c > 0 or q > 0
                    if has_state:
                        s_q = carry[:, p, :] if q == 0 else state[:, ub, q - 1, :]
                        nc.tensor.matmul(yb[:, cols], s_q, rsum[:, cols], start=True, stop=False,
                                         skip_group_check=True)
                    for h in range(2):
                        hp = slice(h * HS, (h + 1) * HS)
                        last = nc.tensor.matmul(yb[hp, cols], v[:, q, p * P + h * HS:p * P + (h + 1) * HS],
                                                mt[:, ub, 2 * q + h, :], start=not has_state, stop=True,
                                                skip_group_check=True)
                last.then_inc(y_done, 1)

            pe.wait_ge(consts_loaded, 16 * 5)
            pe.wait_ge(weights_loaded, 16 * 10)
            pe.wait_ge(cleared, 4)
            with pe.Fori(0, B) as b:
                for j in range(TPC):
                    transposes(b, 0, j)
                for j in range(TPC):
                    v_proj(b, 0, j)
                for part in range(9):
                    project(b, 0, part)
                for u in range(U + 1):
                    for l in range(L):
                        if u < U:
                            level(b, u, l)
                        if u + 1 < U:
                            project(b, u + 1, l)
                        if u and l == 1:
                            k_transposes(b, u - 1)
                        if u and l == 4:
                            k_times_v(b, u - 1)
                        if u and l == 6:
                            outputs(b, u - 1)
                        if (u, l) in T_AT:
                            transposes(b, 1, T_AT[u, l])
                        if (u, l) in V_AT:
                            v_proj(b, 1, V_AT[u, l])
                        if (u, l) in O_AT:
                            out_proj(b, 0, O_AT[u, l])
                for j in range(TPC):
                    out_proj(b, 1, j)
                pe.wait_ge(res_done, TT * b + TT)

        @block.scalar
        def _(act):
            def z_tile(b, c, j):
                t = TPC * c + j
                act.wait_ge(transposed, TT * b + t + 1)
                if t >= 2:
                    act.wait_ge(zt_ready, TT * b + t - 1)
                for kk in range(KD):
                    cols = slice(kk * P, (kk + 1) * P)
                    last = nc.scalar.activation(z[:, t % 2, cols], row[j % 2][:, cols], ACT.Identity,
                                                bias=beta[:, kk:kk + 1], scale=gamma[:, kk:kk + 1])
                last.then_inc(z_ready, 1)
                act.wait_ge(z_ready, TT * b + t + 1)
                nc.scalar.activation(zt_hi[:, c, :, j * P:(j + 1) * P],
                                     z[:, t % 2, :].rearrange("p (k t) -> p k t", k=KD), ACT.Copy).then_inc(zhi_ready, 1)

            def v_tile(b, c, j):
                act.wait_ge(v_done, TT * b + TPC * c + j + 1)
                if c:
                    act.wait_ge(y_done, U * b + NPAIR)
                nc.scalar.activation(v[:, j, :], row[j % 2][:, :], ACT.Copy).then_inc(v_ready, 1)

            def projected(b, u, job):
                n, ub, p = 3 * u + job, u % 2, u % NPAIR
                act.wait_ge(proj_done, 3 * U * b + n + 1)
                if job == 0:
                    if u >= 2:
                        act.wait_ge(rsum_ready, U * b + u - 1)
                    for h in range(2):
                        hp = slice(h * HS, (h + 1) * HS)
                        last = nc.scalar.activation(r[hp, ub, h, :], pj[n % 2][hp, :], ACT.Sigmoid)
                elif job == 1:
                    if u >= 2:
                        act.wait_ge(kt_done, U * b + u - 1)
                    last = nc.scalar.activation(k[:, ub, :], pj[n % 2][:, :], ACT.Copy)
                else:
                    if u >= 2:
                        act.wait_ge(state_step, ST * b + states_before(u - 1, 0))
                    last = nc.scalar.activation(decay[:, ub, 0:TC], pj[n % 2][:, :], ACT.Sigmoid,
                                                bias=neg_bw[:, p:p + 1], scale=-1.0)
                last.then_inc(proj_used, 1)

            def ktok_copy(b, u):
                act.wait_ge(kt_done, U * b + u + 1)
                if u:
                    act.wait_ge(kv_done, U * b + u)
                nc.scalar.activation(ktok[:, :], ks[:, :], ACT.Copy).then_inc(ktok_ready, 1)

            def y_hi(b, u):
                act.wait_ge(y_done, U * b + u + 1)
                if u >= NPAIR:
                    act.wait_ge(out_done, TT * b + TPC)
                nc.scalar.activation(yt_hi[:, u % NPAIR, :], yb[:, :], ACT.Copy).then_inc(yhi_ready, 1)

            act.wait_ge(consts_loaded, 16 * 5)
            act.wait_ge(cleared, 4)
            act.wait_ge(negated, 1)
            with act.Fori(0, B) as b:
                for j in range(TPC):
                    z_tile(b, 0, j)
                for j in range(TPC):
                    v_tile(b, 0, j)
                for job in range(3):
                    projected(b, 0, job)
                for u in range(U + 1):
                    for l in range(L):
                        if u + 1 < U and l % 3 == 2:
                            projected(b, u + 1, l // 3)
                        if u and l == 2:
                            ktok_copy(b, u - 1)
                        if u and l == 7:
                            y_hi(b, u - 1)
                        if (u, l) in T_AT:
                            z_tile(b, 1, T_AT[u, l])
                        if (u, l) in V_AT:
                            v_tile(b, 1, V_AT[u, l])
                act.wait_ge(res_done, TT * b + TT)

        @block.vector
        def _(dve):
            steps = [0]

            def norm_stats(b, c):
                def count():
                    steps[0] += 1
                    return LN * b + steps[0]

                def then(op):
                    op.then_inc(ln_step, 1)
                    dve.wait_ge(ln_step, count())
                dve.wait_ge(x_loaded[c], 16 * b + 16)
                for j in range(TPC):
                    nc.vector.bn_stats(stats[:, j, :], x[:, c, j, :]).then_inc(ln_step, 1)
                    count()
                dve.wait_ge(ln_step, LN * b + steps[0])
                dve.sem_inc(waited, 1)
                for j in range(TPC):
                    nc.vector.bn_aggr(mv[:, j, :], stats[:, j, :]).then_inc(ln_step, 1)
                    count()
                dve.wait_ge(ln_step, LN * b + steps[0])
                then(nc.vector.tensor_scalar(var[:, :], mv[:, :, 1], EPS, None, ALU.add))
                rsqrt_newton(nc, dve, ln_step, count, var[:, :], rstd[:, :], tmp[:, :])
                then(nc.vector.tensor_tensor(var2[:, :], rstd[:, :], rstd[:, :], ALU.mult))
                then(nc.vector.tensor_tensor(var2[:, :], var2[:, :], mv[:, :, 1], ALU.mult))
                then(nc.vector.tensor_scalar(var2[:, :], var2[:, :], EPS, None, ALU.add))
                rsqrt_newton(nc, dve, ln_step, count, var2[:, :], rstd2[:, :], tmp[:, :])
                then(nc.vector.tensor_tensor(rstd[:, :], rstd[:, :], rstd2[:, :], ALU.mult))

            def normed(b, c, j):
                t = TPC * c + j
                if t >= 2:
                    dve.wait_ge(transposed, TT * b + t - 1)
                nc.vector.tensor_scalar(xn[:, t % 2, :], x[:, c, j, :], mv[:, j, 0:1], rstd[:, j:j + 1],
                                        ALU.subtract, ALU.mult).then_inc(xn_ready, 1)

            def z_lo(b, c, j):
                t = TPC * c + j
                dve.wait_ge(zhi_ready, TT * b + t + 1)
                cols = slice(j * P, (j + 1) * P)
                nc.vector.tensor_tensor(zt_lo[:, c, :, cols], z[:, t % 2, :].rearrange("p (k t) -> p k t", k=KD),
                                        zt_hi[:, c, :, cols], ALU.subtract).then_inc(zt_ready, 1)

            def update(b, u, g):
                ub = u % 2
                if g == 0:
                    dve.wait_ge(lv_done, L * U * b + L * u + 2)
                    dve.wait_ge(proj_used, 3 * U * b + 3 * u + 3)
                    for h in range(2):
                        hp = slice(h * HS, (h + 1) * HS)
                        last = nc.vector.tensor_tensor(r[hp, ub, h, :], r[hp, ub, h, :], decay[hp, ub, 0:TC], ALU.mult)
                    last.then_inc(updated, 1)
                    return
                m = LEVELS[g - 1]
                n = TC // (2 * m)
                dve.wait_ge(lv_done, L * U * b + L * u + g + 2)
                dve.wait_ge(updated, UPD * U * b + UPD * u + g)
                total = decay[:, ub, OFF[g - 1]:OFF[g - 1] + TC // m].rearrange("p (n two) -> p n two", two=2)
                for h in range(2):
                    hp = slice(h * HS, (h + 1) * HS)
                    right = r[hp, ub, h, :].rearrange("p (n two m) -> p n two m", two=2, m=m)[:, :, 1, :]
                    nc.vector.tensor_tensor(right, right, total[hp, :, 0:1].to_broadcast([HS, n, m]), ALU.mult)
                left = k[:, ub, :].rearrange("p (n two m) -> p n two m", two=2, m=m)[:, :, 0, :]
                nc.vector.tensor_tensor(left, left, total[:, :, 1:2].to_broadcast([P, n, m]), ALU.mult)
                nc.vector.tensor_tensor(decay[:, ub, OFF[g]:OFF[g] + n], total[:, :, 0], total[:, :, 1],
                                        ALU.mult).then_inc(updated, 1)

            def keep_scores(b, u, l):
                n, ub = L * u + l, u % 2
                dve.wait_ge(lv_done, L * U * b + n + 1)
                if l == 0 and u >= 2:
                    dve.wait_ge(y_done, U * b + u - 1)
                if l:
                    dve.wait_ge(lv_used, L * U * b + n)
                if l < 2:
                    out = mt[:, ub, 4 * l:4 * l + 4, :]
                    src = lv[n % 2][:, :].rearrange("p (g t) -> p g t", g=4)
                    mask = masks[:, 0:1, :].to_broadcast([P, 4, P])
                else:
                    m = LEVELS[l - 2]
                    nb = P // (2 * m)
                    out = mt[:, ub, :, :].rearrange("p g (n two m) -> p g n two m", two=2, m=m)[:, :, :, 1, :]
                    src = lv[n % 2][:, :].rearrange("p (g n m) -> p g n m", g=2 * Q, m=m)
                    mask = masks[:, l - 1, :].rearrange("p (n two m) -> p n two m", two=2, m=m)[:, :, 1, :]
                    mask = mask.unsqueeze(1).to_broadcast([P, 2 * Q, nb, m])
                dve.sem_inc(waited, 1)
                nc.vector.copy_predicated(out, mask, src).then_inc(lv_used, 1)

            def r_sum(b, u):
                dve.wait_ge(updated, UPD * U * b + UPD * (u + 1))
                if u:
                    dve.wait_ge(y_done, U * b + u)
                nc.vector.tensor_tensor(rsum[:, :], r[:, u % 2, 0, :], r[:, u % 2, 1, :], ALU.add).then_inc(rsum_ready, 1)

            def states(b, u):
                c, p, ub = u // NPAIR, u % NPAIR, u % 2
                dve.wait_ge(kv_done, U * b + u + 1)
                for q in range(Q if c == 0 else Q - 1):
                    if states_before(u, q):
                        dve.wait_ge(state_step, ST * b + states_before(u, q))
                    for h in range(2):
                        hp = slice(h * HS, (h + 1) * HS)
                        new = state[hp, ub, q, hp] if q < Q - 1 else carry[hp, p, hp]
                        old = state[hp, ub, q - 1, hp] if q else carry[hp, p, hp]
                        kv = ks[hp, q * P + h * HS:q * P + (h + 1) * HS]
                        if c == 0 and q == 0:
                            op = nc.vector.tensor_copy(new, kv)
                        else:
                            chunk_decay = decay[hp, ub, OFF[-1] + q:OFF[-1] + q + 1]
                            op = nc.vector.scalar_tensor_tensor(out=new, in0=old, scalar=chunk_decay, in1=kv,
                                                                op0=ALU.mult, op1=ALU.add)
                        op.then_inc(state_step, 1)

            def y_lo(b, u):
                dve.wait_ge(yhi_ready, U * b + u + 1)
                nc.vector.tensor_tensor(yt_lo[:, u % NPAIR, :], yb[:, :], yt_hi[:, u % NPAIR, :],
                                        ALU.subtract).then_inc(yt_ready, 1)

            def residual(b, c, j):
                dve.wait_ge(out_done, TT * b + TPC * c + j + 1)
                nc.vector.tensor_tensor(x[:, c, j, :], x[:, c, j, :], row[j % 2][:, :], ALU.add).then_inc(res_done, 1)

            dve.wait_ge(consts_loaded, 16 * 5)
            nc.vector.tensor_scalar(neg_bw[:, :], bw[:, :], -1.0, None, ALU.mult).then_inc(negated, 1)
            dve.wait_ge(cleared, 4)
            with dve.Fori(0, B) as b:
                steps[0] = 0
                norm_stats(b, 0)
                normed(b, 0, 0)
                for j in range(1, TPC):
                    normed(b, 0, j)
                    z_lo(b, 0, j - 1)
                z_lo(b, 0, TPC - 1)
                for u in range(U + 1):
                    if u == 1:
                        norm_stats(b, 1)
                        normed(b, 1, 0)
                        normed(b, 1, 1)
                    for l in range(L):
                        if u < U:
                            if l:
                                update(b, u, l - 1)
                            keep_scores(b, u, l)
                        if u and l == 0:
                            r_sum(b, u - 1)
                        if u and l == 5:
                            states(b, u - 1)
                        if u and l == 7:
                            y_lo(b, u - 1)
                        if (u, l) in T_AT:
                            j = T_AT[u, l]
                            z_lo(b, 1, j)
                            if j + 2 < TPC:
                                normed(b, 1, j + 2)
                        if (u, l) in O_AT:
                            residual(b, 0, O_AT[u, l])
                for j in range(TPC):
                    residual(b, 1, j)
                assert steps[0] == LN


def build(nc, x, w1g, w3g, w2t, wxt, ww, wk, wv, wr, wo, bw, gamma, beta, had, ident, masks, out):
    def scratch(name, shape, dt=F32):
        return nc.dram_tensor(name, shape, dt, kind="Internal").ap()
    w2p = scratch("w2p", [NG, P, HT, D])
    attn_hi = scratch("attn_hi", [5, P, KD, D])
    attn_lo = scratch("attn_lo", [5, P, KD, D])
    x1 = scratch("x1", [B * T, D])
    x2 = scratch("x2", [B * T, D])
    prepare_weights(nc, w2t, wxt, (ww, wk, wv, wr, wo), had, w2p, attn_hi, attn_lo)
    feed_forward(nc, "ffn1", x, x1, w1g, w3g, w2p, ident)
    mixing(nc, x1, x2, attn_hi, attn_lo, gamma, beta, bw, ident, masks)
    feed_forward(nc, "ffn2", x2, out, w1g, w3g, w2p, ident)


def kernel(**inputs):
    import numpy as np
    import concourse.bacc as bacc
    from concourse.bass_utils import run_bass_kernel_spmd

    arr = {n: np.asarray(a) for n, a in inputs.items()}
    up = lambda w: np.ascontiguousarray(w.reshape(NG, GH, KD, P).transpose(0, 3, 2, 1))
    cols = lambda v: np.ascontiguousarray(v.reshape(KD, P).T)
    i = np.arange(P)
    bits = i[:, None] & i[None, :]
    odd = sum((bits >> n) & 1 for n in range(7)) & 1
    s, t = i[:, None], i[None, :]
    masks = [s == t] + [(s // (2 * m) == t // (2 * m)) & (s % (2 * m) < m) & (t % (2 * m) >= m) for m in LEVELS]
    data = {
        "x": arr["L0_attn_x"].reshape(B * T, D),
        "w1g": up(arr["L0_ffn_W1"]),
        "w3g": up(arr["L0_ffn_W3"]),
        "w2t": np.ascontiguousarray(arr["L0_ffn_W2"].T),
        "wxt": np.ascontiguousarray(arr["L0_attn_Wx"].T),
        "ww": arr["L0_attn_Ww"],
        "wk": arr["L0_attn_Wk"],
        "wv": arr["L0_attn_Wv"],
        "wr": arr["L0_attn_Wr"],
        "wo": arr["L0_attn_Wout"],
        "bw": cols(arr["L0_attn_bw"]),
        "gamma": cols(arr["L0_attn_gamma"]),
        "beta": cols(arr["L0_attn_beta"]),
        "had": np.where(odd == 1, -1.0, 1.0).astype(np.float32),
        "ident": np.eye(P, dtype=np.float32),
        "masks": np.ascontiguousarray(np.stack(masks, 1).astype(np.int32)),
    }
    nc = bacc.Bacc("TRN2", target_bir_lowering=False, num_devices=1)
    aps = {n: nc.dram_tensor(f"in_{n}", a.shape, mybir.dt.from_np(a.dtype), kind="ExternalInput").ap()
           for n, a in data.items()}
    out = nc.dram_tensor("out_x", (B * T, D), F32, kind="ExternalOutput").ap()
    build(nc, **aps, out=out)
    res = run_bass_kernel_spmd(nc, [{f"in_{n}": a for n, a in data.items()}], core_ids=[0])
    return res.results[0]["out_x"].reshape(B, T, D)
```

```python
import concourse.bass as bass
from concourse import mybir
from contextlib import ExitStack

F32 = mybir.dt.float32
F32R = mybir.dt.float32r
I32 = mybir.dt.int32
ALU = mybir.AluOpType
ACT = mybir.ActivationFunctionType

P = 128
B, T, D, H = 2, 1024, 512, 2048
NT = B * T // P
KD = D // P
TC = 512
NC = B * T // TC
TPC = TC // P
GH = 256
NG = H // GH
HT = GH // P
EPS = 1e-5
HS = 64
NPAIR = D // P
LEVELS = [1, 2, 4, 8, 16, 32, 64]
MAGIC = 0x5F3759DF


class Rsqrt:

    def __init__(self, nc, dve, step, count, v, y, t, half):
        self.nc, self.dve, self.step, self.count = nc, dve, step, count
        self.v, self.y, self.t, self.half = v, y, t, half

    def then(self, op):
        op.then_inc(self.step, 1)
        self.dve.wait_ge(self.step, self.count())

    def guess(self):
        vector = self.nc.vector
        self.then(vector.tensor_scalar(self.half, self.v, -0.5, None, ALU.mult))
        self.then(vector.tensor_scalar(self.t.bitcast(I32), self.v.bitcast(I32), 1, None, ALU.logical_shift_right))
        self.then(vector.tensor_scalar(self.y.bitcast(I32), self.t.bitcast(I32), -1.0, float(MAGIC), ALU.mult, ALU.add))

    def improve(self):
        vector = self.nc.vector
        self.then(vector.tensor_tensor(self.t, self.y, self.y, ALU.mult))
        self.then(vector.tensor_tensor(self.t, self.t, self.half, ALU.mult))
        self.then(vector.scalar_tensor_tensor(out=self.y, in0=self.t, scalar=1.5, in1=self.y, op0=ALU.add, op1=ALU.mult))


def prepare_weights(nc, w2t, wxt, ww, wo, had, w2p, wxw, wo_hi, wo_lo):
    NB = H // P
    STAGES = 3
    DQ = D // 4
    QT = 4
    with ExitStack() as ctx:
        def sb(name, shape, dt=F32):
            return ctx.enter_context(nc.sbuf_tensor(name, shape, dt))

        def sem(name):
            return ctx.enter_context(nc.semaphore(name))
        fly = sb("fly", [P, 4, NB, DQ])
        other = sb("other", [P, 2, NB, DQ])
        had_sb = sb("had_sb", [P, 2, P])
        wx_sb = sb("wx_sb", [P, KD, D])
        ww_sb = sb("ww_sb", [P, KD, D])
        wxw_sb = sb("wxw_sb", [P, KD, D])
        wo_sb = sb("wo_sb", [P, KD, D])
        wo_hi_sb = sb("wo_hi_sb", [P, KD, D], F32R)
        wo_lo_sb = sb("wo_lo_sb", [P, KD, D], F32R)
        w2o = sb("w2o", [P, 2, NB, DQ])
        ps = [ctx.enter_context(nc.psum_tensor(f"prep_ps{i}", [P, D], F32)) for i in range(4)]
        w2_loaded = [sem(f"w2_loaded{q}") for q in range(4)]
        had_loaded = sem("had_loaded")
        wx_loaded = sem("wx_loaded")
        wo_loaded = sem("wo_loaded")
        flown = sem("flown")
        prod = sem("prod")
        copied = sem("copied")
        w2_stored = [sem(f"w2_stored{i}") for i in range(2)]
        wo_split = sem("wo_split")
        wo_hi_ready = sem("wo_hi_ready")
        small_stored = sem("small_stored")
        block = ctx.enter_context(nc.Block())

        @block.sync
        def _(sp):
            w2_v = w2t.rearrange("(b p) d -> p b d", p=P)
            w2p_v = w2p.rearrange("g p h d -> p g h d")
            for q in range(4):
                sp.dma_start(fly[:, q, :, :], w2_v[:, :, q * DQ:(q + 1) * DQ]).then_inc(w2_loaded[q], 16)
                if q == 0:
                    sp.dma_start(had_sb[:, :, :], had).then_inc(had_loaded, 16)
                if q == 1:
                    sp.dma_start(wx_sb[:, :, :], wxt.rearrange("(k p) d -> p k d", p=P)).then_inc(wx_loaded, 16)
                    sp.dma_start(ww_sb[:, :, :], ww.rearrange("(k p) d -> p k d", p=P)).then_inc(wx_loaded, 16)
            sp.dma_start(wo_sb[:, :, :], wo.rearrange("(k p) d -> p k d", p=P)).then_inc(wo_loaded, 16)
            for q in range(4):
                sp.wait_ge(copied, 4 * (q + 1))
                for h in range(HT):
                    sp.dma_start(w2p_v[:, :, h, q * DQ:(q + 1) * DQ],
                                 w2o[:, q % 2, :, :].rearrange("p (g h) d -> p g h d", h=HT)[:, :, h, :]
                                 ).then_inc(w2_stored[q % 2], 16)
                if q == 2:
                    sp.wait_ge(wo_split, 1)
                    sp.dma_start(wo_hi, wo_hi_sb[:, :, :].bitcast(F32)).then_inc(small_stored, 16)
                    sp.dma_start(wo_lo, wo_lo_sb[:, :, :].bitcast(F32)).then_inc(small_stored, 16)
            sp.wait_ge(copied, 16 + KD)
            sp.dma_start(wxw, wxw_sb[:, :, :]).then_inc(small_stored, 16)
            for i in range(2):
                sp.wait_ge(w2_stored[i], 16 * HT * 2)
            sp.wait_ge(small_stored, 16 * 3)

        @block.vector
        def _(dve):
            for q in range(4):
                dve.wait_ge(w2_loaded[q], 16)
                if q >= 2:
                    dve.wait_ge(prod, 4 * (q - 1))
                pair = (fly[:, q], other[:, q % 2])
                for s in range(STAGES):
                    if s:
                        dve.wait_ge(flown, 2 * STAGES * q + 2 * s)
                    src, dst = (pair[(s + i) % 2].rearrange("p (n two h) d -> p n two (h d)", two=2, h=1 << s)
                                for i in range(2))
                    nc.vector.tensor_tensor(dst[:, :, 0], src[:, :, 0], src[:, :, 1], ALU.add).then_inc(flown, 1)
                    nc.vector.tensor_tensor(dst[:, :, 1], src[:, :, 0], src[:, :, 1], ALU.subtract).then_inc(flown, 1)

        @block.gpsimd
        def _(pool):
            pool.wait_ge(wo_hi_ready, 1)
            nc.gpsimd.tensor_tensor(wo_lo_sb[:, :, :], wo_sb[:, :, :], wo_hi_sb[:, :, :], ALU.subtract).then_inc(wo_split, 1)

        @block.tensor
        def _(pe):
            pe.wait_ge(had_loaded, 16)
            for q in range(4):
                pe.wait_ge(flown, 2 * STAGES * (q + 1))
                for part in range(4):
                    if q:
                        pe.wait_ge(copied, 4 * (q - 1) + part + 1)
                    low = QT * (part % 2)
                    for half in range(2):
                        tiles = slice(low + half * NB // 2, low + half * NB // 2 + QT)
                        sign = 1 if part >= 2 and half else 0
                        last = nc.tensor.matmul(ps[part][:, :], had_sb[:, sign, :], other[:, q % 2, tiles, :],
                                                start=(half == 0), stop=(half == 1))
                    last.then_inc(prod, 1)
            pe.wait_ge(wx_loaded, 32)
            for m in range(KD):
                pe.wait_ge(copied, 12 + m + 1)
                for k in range(KD):
                    last = nc.tensor.matmul(ps[m][:, :], wx_sb[:, k, m * P:(m + 1) * P], ww_sb[:, k, :],
                                            start=(k == 0), stop=(k == KD - 1))
                last.then_inc(prod, 1)

        @block.scalar
        def _(act):
            for q in range(4):
                if q >= 2:
                    act.wait_ge(w2_stored[q % 2], 16 * HT)
                if q == 2:
                    act.wait_ge(wo_loaded, 16)
                    nc.scalar.activation(wo_hi_sb[:, :, :], wo_sb[:, :, :], ACT.Copy).then_inc(wo_hi_ready, 1)
                for part in range(4):
                    act.wait_ge(prod, 4 * q + part + 1)
                    nc.scalar.activation(w2o[:, q % 2, QT * part:QT * part + QT, :], ps[part][:, :], ACT.Copy,
                                         scale=0.5 / H ** 0.5).then_inc(copied, 1)
            for m in range(KD):
                act.wait_ge(prod, 16 + m + 1)
                nc.scalar.activation(wxw_sb[:, m, :], ps[m][:, :], ACT.Copy).then_inc(copied, 1)


def feed_forward(nc, tag, x_in, x_out, w1g, w3g, w2p, ident_in):
    with ExitStack() as ctx:
        def sb(name, shape, dt=F32):
            return ctx.enter_context(nc.sbuf_tensor(f"{tag}_{name}", shape, dt))

        def sem(name):
            return ctx.enter_context(nc.semaphore(f"{tag}_{name}"))
        x = sb("x", [P, NT, D])
        xt_hi = sb("xt_hi", [P, KD, NC * TC], F32R)
        xt_lo = sb("xt_lo", [P, KD, NC * TC], F32R)
        raw1 = sb("raw1", [P, 2, KD, GH])
        raw3 = sb("raw3", [P, 2, KD, GH])
        raw2 = sb("raw2", [P, 2, HT, D])
        w1_hi = sb("w1_hi", [P, 2, KD, GH], F32R)
        w1_lo = sb("w1_lo", [P, 2, KD, GH], F32R)
        w3_hi = sb("w3_hi", [P, 2, KD, GH], F32R)
        w3_lo = sb("w3_lo", [P, 2, KD, GH], F32R)
        w2_hi = sb("w2_hi", [P, 2, HT, D], F32R)
        w2_lo = sb("w2_lo", [P, 2, HT, D], F32R)
        silu = sb("silu", [P, 2, TC])
        hid = sb("hid", [P, 2, TC])
        hid_hi = sb("hid_hi", [P, 2, HT, TC], F32R)
        hid_lo = sb("hid_lo", [P, 2, HT, TC], F32R)
        xn = sb("xn", [P, TPC, D])
        stats = sb("stats", [P, TPC, 6])
        mv = sb("mv", [P, TPC, 2])
        var = sb("var", [P, TPC])
        rstd = sb("rstd", [P, TPC])
        half = sb("half", [P, TPC])
        tmp = sb("tmp", [P, TPC])
        ident = sb("ident", [P, P])

        def bank(name):
            return ctx.enter_context(nc.psum_tensor(f"{tag}_{name}", [P, TC], F32))
        gate = [bank(f"gate{i}") for i in range(HT)]
        lin = [bank(f"lin{i}") for i in range(HT)]
        down = [bank(f"down{i}") for i in range(TPC)]

        ident_loaded = sem("ident_loaded")
        x_loaded = [sem(f"x_loaded{c}") for c in range(NC)]
        raw_loaded = [[sem(f"raw{m}_loaded{b}") for b in range(2)] for m in (1, 3, 2)]
        weights_hi = sem("weights_hi")
        weights_lo = sem("weights_lo")
        ln_step = sem("ln_step")
        xn_ready = sem("xn_ready")
        transposed = sem("transposed")
        xt_hi_ready = sem("xt_hi_ready")
        xt_ready = sem("xt_ready")
        gate_done = sem("gate_done")
        lin_done = sem("lin_done")
        silu_done = sem("silu_done")
        hid_done = sem("hid_done")
        hi_done = sem("hi_done")
        lo_done = sem("lo_done")
        down_done = sem("down_done")
        added = sem("added")
        stored = sem("stored")
        block = ctx.enter_context(nc.Block())
        STEPS = NG * NC
        PER = 2 * NC

        xin_v = x_in.rearrange("(n p) d -> p n d", p=P)
        xout_v = x_out.rearrange("(n p) d -> p n d", p=P)

        @block.sync
        def _(sp):
            sp.dma_start(ident[:, :], ident_in).then_inc(ident_loaded, 16)

            def load_group(g, b):
                sp.dma_start(raw1[:, b, :, :], w1g[g]).then_inc(raw_loaded[0][b], 16)
                sp.dma_start(raw3[:, b, :, :], w3g[g]).then_inc(raw_loaded[1][b], 16)
                sp.dma_start(raw2[:, b, :, :], w2p[g]).then_inc(raw_loaded[2][b], 16)
            for c in range(NC):
                sp.dma_start(x[:, c * TPC:(c + 1) * TPC, :],
                             xin_v[:, c * TPC:(c + 1) * TPC, :]).then_inc(x_loaded[c], 16)
                if c < 2:
                    load_group(c, c)
            with sp.Fori(1, NG // 2) as i:
                for b in range(2):
                    sp.wait_ge(weights_lo, 6 * i + 3 * b - 3)
                    load_group(2 * i + b, b)
            for t in range(NT):
                sp.wait_ge(added, (STEPS - NC) * TPC + t + 1)
                sp.dma_start(xout_v[:, t, :], x[:, t, :]).then_inc(stored, 16)
            sp.wait_ge(stored, 16 * NT)

        @block.gpsimd
        def _(pool):
            def low_parts(g3, b):
                for n, (raw, hi, lo) in enumerate(((raw1, w1_hi, w1_lo), (raw3, w3_hi, w3_lo), (raw2, w2_hi, w2_lo))):
                    pool.wait_ge(weights_hi, g3 + n + 1)
                    nc.gpsimd.tensor_tensor(lo[:, b], raw[:, b], hi[:, b], ALU.subtract).then_inc(weights_lo, 1)
            for b in range(2):
                low_parts(3 * b, b)
            with pool.Fori(1, NG // 2) as i:
                for b in range(2):
                    low_parts(6 * i + 3 * b, b)

        @block.tensor
        def _(pe):
            def transposes(c, free):
                for j in range(TPC):
                    t = c * TPC + j
                    pe.wait_ge(xn_ready, t + 1)
                    free(j)
                    for k in range(KD):
                        cols = slice(k * P, (k + 1) * P)
                        last = nc.tensor.transpose(down[j][:, cols], xn[:, j, cols], ident[:, :])
                    last.then_inc(transposed, 1)

            def up(n, j, h, group3):
                b, c = (j // NC) % 2, j % NC
                cols, xs = slice(h * P, (h + 1) * P), slice(c * TC, (c + 1) * TC)
                for m, (psum, hi, lo, done, used) in enumerate(((gate[h], w1_hi, w1_lo, gate_done, silu_done),
                                                                (lin[h], w3_hi, w3_lo, lin_done, hid_done))):
                    if c == 0 and h == 0:
                        pe.wait_ge(weights_lo, group3 + m + 1)
                    if not (isinstance(n, int) and n == 0):
                        pe.wait_ge(used, HT * n + h - 1)
                    for k in range(KD):
                        nc.tensor.matmul(psum[:, :], hi[:, b, k, cols], xt_hi[:, k, xs], start=(k == 0), stop=False)
                        nc.tensor.matmul(psum[:, :], hi[:, b, k, cols], xt_lo[:, k, xs], start=False, stop=False)
                        last = nc.tensor.matmul(psum[:, :], lo[:, b, k, cols], xt_hi[:, k, xs],
                                                start=False, stop=(k == KD - 1))
                    last.then_inc(done, 1)

            def downs(n, j, group3, free):
                b, s = (j // NC) % 2, j % 2
                if j % NC == 0:
                    pe.wait_ge(weights_lo, group3 + 3)
                pe.wait_ge(lo_done, HT * n + HT)
                for t in range(TPC):
                    free(t)
                    cols = slice(t * P, (t + 1) * P)
                    for h in range(HT):
                        nc.tensor.matmul(down[t][:, :], hid_hi[:, s, h, cols], w2_hi[:, b, h, :], start=(h == 0), stop=False)
                        nc.tensor.matmul(down[t][:, :], hid_hi[:, s, h, cols], w2_lo[:, b, h, :], start=False, stop=False)
                        last = nc.tensor.matmul(down[t][:, :], hid_lo[:, s, h, cols], w2_hi[:, b, h, :],
                                                start=False, stop=(h == HT - 1))
                    last.then_inc(down_done, 1)

            def banks_added(n):
                return lambda t: pe.wait_ge(added, TPC * n - TPC + t + 1)

            def lo_written(c):
                return lambda t: pe.wait_ge(xt_ready, TPC * c + t + 1)

            pe.wait_ge(ident_loaded, 16)
            transposes(0, lambda j: None)
            for n in range(PER):
                g3 = 3 * (n // NC)
                if n < NC:
                    pe.wait_ge(xt_ready, TPC * (n + 1))
                up(n, n, 0, g3)
                if n + 1 < NC:
                    transposes(n + 1, lo_written(n) if n < 2 else lambda j: pe.wait_ge(added, TPC * (n - 2) + j + 1))
                up(n, n, 1, g3)
                if n:
                    downs(n - 1, n - 1, 3 * ((n - 1) // NC), lo_written(n + 1) if n + 1 < NC else
                          lo_written(NC - 1) if n < 3 else banks_added(n - 1))
            with pe.Fori(1, NG // 2) as i:
                for j in range(PER):
                    for h in range(HT):
                        up(PER * i + j, j, h, 6 * i + 3 * (j // NC))
                    downs(PER * i + (j - 1), (j - 1) % PER, 6 * i + (3 * ((j - 1) // NC) if j else -3),
                          banks_added(PER * i + (j - 1)))
            downs(STEPS - 1, PER - 1, 3 * (NG - 1), banks_added(STEPS - 1))

        @block.scalar
        def _(act):
            def transposed_hi(c):
                for j in range(TPC):
                    t = c * TPC + j
                    act.wait_ge(transposed, t + 1)
                    nc.scalar.activation(xt_hi[:, :, t * P:(t + 1) * P],
                                         down[j][:, :].rearrange("p (k t) -> p k t", k=KD), ACT.Copy).then_inc(xt_hi_ready, 1)

            def hidden_tile(n, j, h):
                act.wait_ge(gate_done, HT * n + h + 1)
                if not (isinstance(n, int) and n == 0):
                    act.wait_ge(hid_done, HT * n + h - 1)
                nc.scalar.activation(silu[:, h, :], gate[h][:, :], ACT.Silu).then_inc(silu_done, 1)
                act.wait_ge(hid_done, HT * n + h + 1)
                if not (isinstance(n, int) and n < 2):
                    act.wait_ge(down_done, TPC * n - TPC)
                nc.scalar.activation(hid_hi[:, j % 2, h, :], hid[:, h, :], ACT.Copy).then_inc(hi_done, 1)

            def hidden(n, j):
                for h in range(HT):
                    hidden_tile(n, j, h)

            def high_parts(g3, b, loads, free):
                act.wait_ge(raw_loaded[0][b], loads)
                if free is not None:
                    act.wait_ge(down_done, free)
                for n, (raw, hi) in enumerate(((raw1, w1_hi), (raw3, w3_hi), (raw2, w2_hi))):
                    if n:
                        act.wait_ge(raw_loaded[n][b], loads)
                    nc.scalar.activation(hi[:, b], raw[:, b], ACT.Copy).then_inc(weights_hi, 1)

            def turn(i):
                last = isinstance(i, int) and i == NG // 2 - 1
                for j in range(PER):
                    hidden(PER * i + j, j)
                    if j == 1:
                        high_parts(0, 1, 16 * i + 16, (2 * i) * NC * TPC)
                    if j == NC + 1 and not last:
                        high_parts(0, 0, 16 * i + 32, (2 * i + 1) * NC * TPC)

            high_parts(0, 0, 16, None)
            transposed_hi(0)
            for n in range(PER):
                if n + 1 < NC:
                    hidden_tile(n, n, 0)
                    transposed_hi(n + 1)
                    hidden_tile(n, n, 1)
                else:
                    hidden(n, n)
                if n == 1:
                    high_parts(3, 1, 16, None)
                if n == NC + 1:
                    high_parts(6, 0, 32, NC * TPC)
            with act.Fori(1, NG // 2 - 1) as i:
                turn(i)
            turn(NG // 2 - 1)

        @block.vector
        def _(dve):
            steps = [0]

            def count():
                steps[0] += 1
                return steps[0]

            def then(op):
                op.then_inc(ln_step, 1)
                dve.wait_ge(ln_step, count())

            def norm_stats(c):
                dve.wait_ge(x_loaded[c], 16)
                for j in range(TPC):
                    nc.vector.bn_stats(stats[:, j, :], x[:, c * TPC + j, :]).then_inc(ln_step, 1)
                    count()
                dve.wait_ge(ln_step, steps[0])
                for j in range(TPC):
                    nc.vector.bn_aggr(mv[:, j, :], stats[:, j, :]).then_inc(ln_step, 1)
                    count()
                dve.wait_ge(ln_step, steps[0])
                then(nc.vector.tensor_scalar(var[:, :], mv[:, :, 1], EPS, None, ALU.add))
                root = Rsqrt(nc, dve, ln_step, count, var[:, :], rstd[:, :], tmp[:, :], half[:, :])
                root.guess()
                for _ in range(3):
                    root.improve()
                for j in range(TPC):
                    t = c * TPC + j
                    if c:
                        dve.wait_ge(transposed, t - TPC + 1)
                    nc.vector.tensor_scalar(xn[:, j, :], x[:, t, :], mv[:, j, 0:1], rstd[:, j:j + 1],
                                            ALU.subtract, ALU.mult).then_inc(xn_ready, 1)

            def transposed_lo(c):
                for j in range(TPC):
                    t = c * TPC + j
                    dve.wait_ge(xt_hi_ready, t + 1)
                    cols = slice(t * P, (t + 1) * P)
                    nc.vector.tensor_tensor(xt_lo[:, :, cols], down[j][:, :].rearrange("p (k t) -> p k t", k=KD),
                                            xt_hi[:, :, cols], ALU.subtract).then_inc(xt_ready, 1)

            def hidden_tile(n, j, h):
                dve.wait_ge(silu_done, HT * n + h + 1)
                dve.wait_ge(lin_done, HT * n + h + 1)
                if not (isinstance(n, int) and n == 0):
                    dve.wait_ge(lo_done, HT * n + h - 1)
                nc.vector.tensor_tensor(hid[:, h, :], silu[:, h, :], lin[h][:, :], ALU.mult).then_inc(hid_done, 1)
                dve.wait_ge(hi_done, HT * n + h + 1)
                nc.vector.tensor_tensor(hid_lo[:, j % 2, h, :], hid[:, h, :], hid_hi[:, j % 2, h, :],
                                        ALU.subtract).then_inc(lo_done, 1)

            def hidden(n, j):
                for h in range(HT):
                    hidden_tile(n, j, h)

            def add(n, j, before):
                c = j % NC
                for t in range(TPC):
                    dve.wait_ge(down_done, TPC * n + t + 1)
                    if before:
                        dve.wait_ge(added, TPC * n - NC * TPC + t + 1)
                    xt = x[:, c * TPC + t, :]
                    nc.vector.tensor_tensor(xt, xt, down[t][:, :], ALU.add).then_inc(added, 1)
            norm_stats(0)
            transposed_lo(0)
            for n in range(PER):
                if n + 1 < NC:
                    norm_stats(n + 1)
                    hidden_tile(n, n, 0)
                    transposed_lo(n + 1)
                    hidden_tile(n, n, 1)
                else:
                    hidden(n, n)
                if n >= 1:
                    add(n - 1, n - 1, n - 1 >= NC)
            with dve.Fori(1, NG // 2) as i:
                for j in range(PER):
                    hidden(PER * i + j, j)
                    add(PER * i + (j - 1), (j - 1) % PER, True)
            add(STEPS - 1, PER - 1, True)


def mixing(nc, x_in, x_out, wr_in, wk_in, wv_in, wxw_in, wo_hi_in, wo_lo_in, gamma_in, beta_in, bw_in, ident_in, masks_in):
    NU = NC * NPAIR
    CPB = T // TC
    Q = TC // P
    L = 2 + len(LEVELS)
    UPD = 1 + len(LEVELS)
    ON_DVE = 6
    ON_ACT = L - ON_DVE
    OFF = [2 * TC - (2 * TC >> i) for i in range(len(LEVELS) + 1)]
    SPC = NPAIR
    NORM_AT = {(u, l): L * u + l for u in range(2) for l in range(L) if L * u + l < 15}
    T_AT = {(1, 6): 0, (1, 8): 1, (2, 1): 2, (2, 3): 3}
    V_AT = {(2, 6): 0, (3, 1): 1, (3, 5): 2, (4, 1): 3}
    V0_AT = {(0, 1): 0, (0, 3): 1, (0, 5): 2, (0, 7): 3}
    O_AT = {(4, 8): 0, (5, 1): 1, (5, 3): 2, (5, 5): 3}

    def tiles_at(table, u, l):
        for (du, dl), j in table.items():
            if dl == l and (u - du) % SPC == 0 and 0 <= (u - du) // SPC < NC:
                yield (u - du) // SPC, j

    with ExitStack() as ctx:
        def sb(name, shape, dt=F32):
            return ctx.enter_context(nc.sbuf_tensor(f"mix_{name}", shape, dt))

        def sem(name):
            return ctx.enter_context(nc.semaphore(f"mix_{name}"))
        names = ("wv", "wr", "wk", "wxw", "wo")
        w_hi = [sb(f"{n}_hi", [P, KD, D], F32R) for n in names]
        w_lo = [sb(f"{n}_lo", [P, KD, D], F32R) for n in names]
        WV, WR, WK, WXW, WO = range(5)
        x = sb("x", [P, TPC, D])
        xres = sb("xres", [P, 2, D])
        xn = sb("xn", [P, 2, D])
        z = sb("z", [P, 2, D])
        zt_hi = sb("zt_hi", [P, 2, KD, TC], F32R)
        zt_lo = sb("zt_lo", [P, 2, KD, TC], F32R)
        v = sb("v", [P, 2, TPC, D])
        r = sb("r", [P, 2, 2, TC])
        k = sb("k", [P, 2, TC])
        decay = sb("decay", [P, 2, 2 * TC])
        rsum = sb("rsum", [P, TC])
        mt = sb("mt", [P, 2, 2 * Q, P])
        ktok = sb("ktok", [P, TC])
        state = sb("state", [P, 2, Q - 1, P])
        carry = sb("carry", [P, B, NPAIR, P])
        yt_hi = sb("yt_hi", [P, NPAIR, TC], F32R)
        yt_lo = sb("yt_lo", [P, NPAIR, TC], F32R)
        masks = sb("masks", [P, ON_DVE - 1, P], I32)
        ident = sb("ident", [P, P])
        gamma = sb("gamma", [P, KD])
        beta = sb("beta", [P, KD])
        bw = sb("bw", [P, KD])
        neg_bw = sb("neg_bw", [P, KD])
        stats = sb("stats", [P, TPC, 6])
        mv = sb("mv", [P, TPC, 2])
        small = sb("small", [P, 6, TPC])
        var, rstd, rstd2, var2, tmp, half = (small[:, i, :] for i in range(6))

        def bank(name):
            return ctx.enter_context(nc.psum_tensor(f"mix_{name}", [P, TC], F32))
        row = [bank(f"row{i}") for i in range(2)]
        pj = [bank(f"pj{i}") for i in range(2)]
        lv = [bank(f"lv{i}") for i in range(2)]
        yb = bank("yb")
        ks = bank("ks")

        consts_loaded = sem("consts_loaded")
        raw_loaded = [sem(f"{n}_loaded") for n in names]
        w_hi_ready = sem("w_hi_ready")
        w_ready = sem("w_ready")
        x_loaded = sem("x_loaded")
        res_loaded = [sem(f"res_loaded{i}") for i in range(2)]
        x_stored = [sem(f"x_stored{i}") for i in range(2)]
        cleared = sem("cleared")
        mt_cleared = sem("mt_cleared")
        negated = sem("negated")
        ln_step = sem("ln_step")
        xn_ready = sem("xn_ready")
        transposed = sem("transposed")
        z_ready = sem("z_ready")
        zhi_ready = sem("zhi_ready")
        zt_ready = sem("zt_ready")
        v_done = sem("v_done")
        v_ready = sem("v_ready")
        proj_done = sem("proj_done")
        proj_used = sem("proj_used")
        lv_done = sem("lv_done")
        kept_dve = sem("kept_dve")
        kept_act = sem("kept_act")
        updated = sem("updated")
        totalled = sem("totalled")
        rsum_left = sem("rsum_left")
        kt_done = sem("kt_done")
        ktok_ready = sem("ktok_ready")
        kv_done = sem("kv_done")
        state_step = sem("state_step")
        carried = sem("carried")
        y_done = sem("y_done")
        yhi_ready = sem("yhi_ready")
        yt_ready = sem("yt_ready")
        out_done = sem("out_done")
        res_done = sem("res_done")
        block = ctx.enter_context(nc.Block())

        xin_v = x_in.rearrange("(b c n p) d -> b c p n d", b=B, c=CPB, p=P)
        xout_v = x_out.rearrange("(b c n p) d -> b c n p d", b=B, c=CPB, p=P)
        raw = [v[:, 0, :, :], v[:, 1, :, :], decay.rearrange("p a (k d) -> p (a k) d", d=D),
               mt.rearrange("p a g t -> p (a g t)").rearrange("p (k d) -> p k d", d=D)]

        @block.sync
        def _(sp):
            def load_x(n):
                sp.dma_start(x[:, :, :], xin_v[n % B, n // B]).then_inc(x_loaded, 16)

            def load_res(n, j):
                sp.dma_start(xres[:, j % 2, :], xin_v[n % B, n // B][:, j, :]).then_inc(res_loaded[j % 2], 16)
            sp.dma_start(ident[:, :], ident_in).then_inc(consts_loaded, 16)
            load_x(0)
            for dst, src in ((gamma[:, :], gamma_in), (beta[:, :], beta_in), (bw[:, :], bw_in),
                             (masks[:, :, :], masks_in)):
                sp.dma_start(dst, src).then_inc(consts_loaded, 16)
            for n, src in ((WR, wr_in), (WK, wk_in)):
                sp.dma_start(raw[n], src.rearrange("(k p) d -> p k d", p=P)).then_inc(raw_loaded[n], 16)
            sp.dma_start(raw[WXW], wxw_in).then_inc(raw_loaded[WXW], 16)
            sp.dma_start(raw[WV], wv_in.rearrange("(k p) d -> p k d", p=P)).then_inc(raw_loaded[WV], 16)
            sp.dma_start(w_hi[WO][:, :, :].bitcast(F32), wo_hi_in).then_inc(raw_loaded[WO], 16)
            sp.dma_start(w_lo[WO][:, :, :].bitcast(F32), wo_lo_in).then_inc(raw_loaded[WO], 16)
            load_res(0, 0)
            load_res(0, 1)
            sp.wait_ge(xn_ready, TPC)
            load_x(1)
            for n in range(NC):
                if n + 2 < NC:
                    sp.wait_ge(xn_ready, TPC * (n + 2))
                    load_x(n + 2)
                for j in range(TPC):
                    t = TPC * n + j
                    sp.wait_ge(res_done, t + 1)
                    sp.dma_start(xout_v[n % B, n // B, j], xres[:, j % 2, :]).then_inc(x_stored[j % 2], 16)
                    if t + 2 < NT:
                        sp.wait_ge(x_stored[j % 2], 16 * (t // 2 + 1))
                        load_res((t + 2) // TPC, (t + 2) % TPC)
            for i in range(2):
                sp.wait_ge(x_stored[i], 16 * NT // 2)

        @block.gpsimd
        def _(pool):
            for t in (r[:, :, :, :], state[:, :, :, :], carry[:, :, :, :]):
                nc.gpsimd.memset(t, 0.0).then_inc(cleared, 1)
            for i, n in enumerate((WR, WK, WXW, WV)):
                pool.wait_ge(w_hi_ready, i + 1)
                nc.gpsimd.tensor_tensor(w_lo[n][:, :, :], raw[n], w_hi[n][:, :, :], ALU.subtract).then_inc(w_ready, 1)
                if n == WXW:
                    pool.wait_ge(w_ready, i + 1)
                    nc.gpsimd.memset(mt[:, :, :, :], 0.0).then_inc(mt_cleared, 1)

        @block.tensor
        def _(pe):
            def three(psum, lhs_hi, lhs_lo, rhs_hi, rhs_lo, start, stop):
                nc.tensor.matmul(psum, lhs_hi, rhs_hi, start=start, stop=False)
                nc.tensor.matmul(psum, lhs_hi, rhs_lo, start=False, stop=False)
                return nc.tensor.matmul(psum, lhs_lo, rhs_hi, start=False, stop=stop)

            def transposes(n, j):
                t = TPC * n + j
                pe.wait_ge(xn_ready, t + 1)
                if j >= 2:
                    pe.wait_ge(z_ready, t - 1)
                elif n >= 2:
                    pe.wait_ge(res_done, TPC * (n - 2) + j + 3)
                elif n:
                    pe.wait_ge(v_ready, j + 3)
                for kk in range(KD):
                    cols = slice(kk * P, (kk + 1) * P)
                    last = nc.tensor.transpose(row[j % 2][:, cols], xn[:, j % 2, cols], ident[:, :])
                last.then_inc(transposed, 1)

            def v_proj(n, j):
                t = TPC * n + j
                pe.wait_ge(zt_ready, t + 1)
                if j >= 2:
                    pe.wait_ge(v_ready, t - 1)
                else:
                    pe.wait_ge(z_ready, TPC * n + j + 3)
                if n == 0:
                    pe.wait_ge(w_ready, 4)
                cols = slice(j * P, (j + 1) * P)
                for kk in range(KD):
                    last = three(row[j % 2][:, :], zt_hi[:, n % 2, kk, cols], zt_lo[:, n % 2, kk, cols],
                                 w_hi[WV][:, kk, :], w_lo[WV][:, kk, :], kk == 0, kk == KD - 1)
                last.then_inc(v_done, 1)

            def out_proj(n, j):
                t = TPC * n + j
                pe.wait_ge(yt_ready, NPAIR * (n + 1))
                if j >= 2:
                    pe.wait_ge(res_done, t - 1)
                elif n + 1 < NC:
                    pe.wait_ge(v_ready, TPC * (n + 1) + j + 3)
                else:
                    pe.wait_ge(res_done, t - 2)
                if n == 0:
                    pe.wait_ge(raw_loaded[WO], 32)
                cols = slice(j * P, (j + 1) * P)
                for kk in range(NPAIR):
                    last = three(row[j % 2][:, :], yt_hi[:, kk, cols], yt_lo[:, kk, cols],
                                 w_hi[WO][:, kk, :], w_lo[WO][:, kk, :], kk == 0, kk == NPAIR - 1)
                last.then_inc(out_done, 1)

            def project(u, part):
                n, p, job, third = u // NPAIR, u % NPAIR, part // 3, part % 3
                i3 = 3 * u + job
                if third == 0:
                    pe.wait_ge(zt_ready, TPC * (n + 1))
                    if i3 >= 2:
                        pe.wait_ge(proj_used, i3 - 1)
                    if u == 0:
                        pe.wait_ge(w_ready, job + 1)
                w = (WR, WK, WXW)[job]
                cols = slice(p * P, (p + 1) * P)
                passes = [(a, e, kk) for kk in range(KD) for a, e in ((w_hi, zt_hi), (w_hi, zt_lo), (w_lo, zt_hi))]
                for i in range(4 * third, 4 * third + 4):
                    a, e, kk = passes[i]
                    last = nc.tensor.matmul(pj[i3 % 2][:, :], a[w][:, kk, cols], e[:, n % 2, kk, :],
                                            start=(i == 0), stop=(i == len(passes) - 1))
                if third == 2:
                    last.then_inc(proj_done, 1)

            def level(u, l):
                i, ub = L * u + l, u % 2
                if i >= 2:
                    pu, pl = (i - 2) // L, (i - 2) % L
                    if pl < ON_DVE:
                        pe.wait_ge(kept_dve, ON_DVE * pu + pl + 1)
                    else:
                        pe.wait_ge(kept_act, ON_ACT * pu + pl - ON_DVE + 1)
                if l == 0:
                    pe.wait_ge(proj_used, 3 * u + 2)
                if l >= 2:
                    pe.wait_ge(updated, UPD * u + l - 1)
                for q in ((2 * l, 2 * l + 1) if l < 2 else range(Q)):
                    cols = slice(q * P, (q + 1) * P)
                    if l < 2:
                        rhs = r[:, ub, :, cols]
                        out = lv[i % 2][:, (q % 2) * 2 * P:(q % 2 + 1) * 2 * P]
                    else:
                        m = LEVELS[l - 2]
                        rhs = r[:, ub, :, cols].rearrange("p h (n two m) -> p h n two m", two=2, m=m)[:, :, :, 1, :]
                        out = lv[i % 2][:, cols]
                    last = nc.tensor.matmul(out, k[:, ub, cols], rhs, start=True, stop=True)
                last.then_inc(lv_done, 1)

            def k_transposes(u):
                pe.wait_ge(updated, UPD * (u + 1))
                if u:
                    pe.wait_ge(carried, 2 * u)
                for q in range(Q):
                    cols = slice(q * P, (q + 1) * P)
                    last = nc.tensor.transpose(ks[:, cols], k[:, u % 2, cols], ident[:, :])
                last.then_inc(kt_done, 1)

            def k_times_v(u):
                n, p = u // NPAIR, u % NPAIR
                pe.wait_ge(ktok_ready, u + 1)
                pe.wait_ge(v_ready, TPC * (n + 1))
                for q in range(Q):
                    cols = slice(q * P, (q + 1) * P)
                    last = nc.tensor.matmul(ks[:, cols], ktok[:, cols], v[:, n % 2, q, p * P:(p + 1) * P],
                                            start=True, stop=True)
                last.then_inc(kv_done, 1)

            def outputs(u):
                n, p, ub = u // NPAIR, u % NPAIR, u % 2
                pe.wait_ge(kept_act, ON_ACT * (u + 1))
                pe.wait_ge(rsum_left, u + 1)
                pe.wait_ge(state_step, 2 * (Q - 1) * (u + 1))
                if u:
                    pe.wait_ge(yt_ready, u)
                for q in range(Q):
                    cols = slice(q * P, (q + 1) * P)
                    s_q = carry[:, n % B, p, :] if q == 0 else state[:, ub, q - 1, :]
                    nc.tensor.matmul(yb[:, cols], s_q, rsum[:, cols], start=True, stop=False, skip_group_check=True)
                    for h in range(2):
                        hp = slice(h * HS, (h + 1) * HS)
                        last = nc.tensor.matmul(yb[hp, cols], v[:, n % 2, q, p * P + h * HS:p * P + (h + 1) * HS],
                                                mt[:, ub, 2 * q + h, :], start=False, stop=True, skip_group_check=True)
                last.then_inc(y_done, 1)

            pe.wait_ge(consts_loaded, 16 * 5)
            pe.wait_ge(cleared, 3)
            for j in range(TPC):
                transposes(0, j)
            for part in range(9):
                project(0, part)
            for u in range(NU + 1):
                for l in range(L):
                    if u < NU:
                        level(u, l)
                    if u + 1 < NU:
                        project(u + 1, l)
                    if u and l == 1:
                        k_transposes(u - 1)
                    if u and l == 4:
                        k_times_v(u - 1)
                    if u and l == 6:
                        outputs(u - 1)
                    if (u, l) in V0_AT:
                        v_proj(0, V0_AT[u, l])
                    for n, j in tiles_at(T_AT, u, l):
                        if n + 1 < NC:
                            transposes(n + 1, j)
                    for n, j in tiles_at(V_AT, u, l):
                        if n + 1 < NC:
                            v_proj(n + 1, j)
                    for n, j in tiles_at(O_AT, u, l):
                        if n + 1 < NC:
                            out_proj(n, j)
            for j in range(TPC):
                out_proj(NC - 1, j)

        @block.scalar
        def _(act):
            def z_tile(n, j):
                t = TPC * n + j
                act.wait_ge(transposed, t + 1)
                if t >= 2:
                    act.wait_ge(zt_ready, t - 1)
                if n >= 2:
                    act.wait_ge(v_done, TPC * (n - 1))
                    act.wait_ge(proj_done, 3 * NPAIR * (n - 1))
                for kk in range(KD):
                    cols = slice(kk * P, (kk + 1) * P)
                    last = nc.scalar.activation(z[:, j % 2, cols], row[j % 2][:, cols], ACT.Identity,
                                                bias=beta[:, kk:kk + 1], scale=gamma[:, kk:kk + 1])
                last.then_inc(z_ready, 1)
                act.wait_ge(z_ready, t + 1)
                nc.scalar.activation(zt_hi[:, n % 2, :, j * P:(j + 1) * P],
                                     z[:, j % 2, :].rearrange("p (k t) -> p k t", k=KD), ACT.Copy).then_inc(zhi_ready, 1)

            def v_tile(n, j):
                act.wait_ge(v_done, TPC * n + j + 1)
                if n >= 2:
                    act.wait_ge(y_done, NPAIR * (n - 1))
                nc.scalar.activation(v[:, n % 2, j, :], row[j % 2][:, :], ACT.Copy).then_inc(v_ready, 1)

            def projected(u, job):
                i3, ub, p = 3 * u + job, u % 2, u % NPAIR
                act.wait_ge(proj_done, i3 + 1)
                if job == 0:
                    if u >= 2:
                        act.wait_ge(updated, UPD * (u - 1))
                        act.wait_ge(rsum_left, u - 1)
                    for h in range(2):
                        hp = slice(h * HS, (h + 1) * HS)
                        last = nc.scalar.activation(r[hp, ub, h, :], pj[i3 % 2][hp, :], ACT.Sigmoid)
                elif job == 1:
                    if u >= 2:
                        act.wait_ge(kt_done, u - 1)
                    last = nc.scalar.activation(k[:, ub, :], pj[i3 % 2][:, :], ACT.Copy)
                else:
                    if u >= 2:
                        act.wait_ge(carried, 2 * (u - 1))
                    if u == 0:
                        act.wait_ge(w_ready, 2)
                    last = nc.scalar.activation(decay[:, ub, 0:TC], pj[i3 % 2][:, :], ACT.Sigmoid,
                                                bias=neg_bw[:, p:p + 1], scale=-1.0)
                last.then_inc(proj_used, 1)

            def keep_scores(u, l):
                i, m, ub = L * u + l, LEVELS[l - 2], u % 2
                act.wait_ge(lv_done, i + 1)
                if l == ON_DVE:
                    act.wait_ge(kept_dve, ON_DVE * (u + 1))
                nb = P // (2 * m)
                out = mt[:, ub, :, :].rearrange("p g (n two m) -> p g n two m", two=2, m=m)
                src = lv[i % 2][:, :].rearrange("p (g n m) -> p g n m", g=2 * Q, m=m)
                for b in range(nb):
                    rows = slice(2 * m * b, 2 * m * b + m)
                    last = nc.scalar.activation(out[rows, :, b, 1, :], src[rows, :, b, :], ACT.Copy)
                last.then_inc(kept_act, 1)

            def sum_left(u):
                act.wait_ge(updated, UPD * u + UPD - 1)
                if u:
                    act.wait_ge(y_done, u)
                for h in range(2):
                    hp = slice(h * HS, (h + 1) * HS)
                    left = [a.rearrange("p (n two m) -> p n two m", two=2, m=HS)[:, :, 0, :]
                            for a in (rsum[hp, :], r[hp, u % 2, h, :])]
                    last = nc.scalar.activation(left[0], left[1], ACT.Copy)
                last.then_inc(rsum_left, 1)

            def ktok_copy(u):
                act.wait_ge(kt_done, u + 1)
                if u:
                    act.wait_ge(kv_done, u)
                nc.scalar.activation(ktok[:, :], ks[:, :], ACT.Copy).then_inc(ktok_ready, 1)

            def y_hi(u):
                act.wait_ge(y_done, u + 1)
                if u >= NPAIR:
                    act.wait_ge(out_done, TPC * (u // NPAIR))
                nc.scalar.activation(yt_hi[:, u % NPAIR, :], yb[:, :], ACT.Copy).then_inc(yhi_ready, 1)

            def high_part(n):
                act.wait_ge(raw_loaded[n], 16)
                nc.scalar.activation(w_hi[n][:, :, :], raw[n], ACT.Copy).then_inc(w_hi_ready, 1)

            high_part(WR)
            high_part(WK)
            act.wait_ge(consts_loaded, 16 * 5)
            for j in range(TPC):
                z_tile(0, j)
            high_part(WXW)
            high_part(WV)
            act.wait_ge(cleared, 3)
            act.wait_ge(negated, 1)
            for job in range(3):
                projected(0, job)
            act.wait_ge(w_ready, 4)
            act.wait_ge(mt_cleared, 1)
            for u in range(NU + 1):
                for l in range(L):
                    if u < NU and l >= ON_DVE:
                        keep_scores(u, l)
                    if u < NU and l == L - 1:
                        sum_left(u)
                    if u + 1 < NU and l % 3 == 2:
                        projected(u + 1, l // 3)
                    if u and l == 2:
                        ktok_copy(u - 1)
                    if u and l == 7:
                        y_hi(u - 1)
                    if (u, l) in V0_AT:
                        v_tile(0, V0_AT[u, l])
                    for n, j in tiles_at(T_AT, u, l):
                        if n + 1 < NC:
                            z_tile(n + 1, j)
                    for n, j in tiles_at(V_AT, u, l):
                        if n + 1 < NC:
                            v_tile(n + 1, j)

        @block.vector
        def _(dve):
            steps = [0]

            def count():
                steps[0] += 1
                return steps[0]

            def then(op):
                op.then_inc(ln_step, 1)
                dve.wait_ge(ln_step, count())

            root = Rsqrt(nc, dve, ln_step, count, var, rstd, tmp, half)
            root2 = Rsqrt(nc, dve, ln_step, count, var2, rstd2, tmp, half)

            def norm(n, part):
                if part < TPC:
                    if part == 0:
                        dve.wait_ge(x_loaded, 16 * (n + 1))
                    then(nc.vector.bn_stats(stats[:, part, :], x[:, part, :]))
                    then(nc.vector.bn_aggr(mv[:, part, :], stats[:, part, :]))
                elif part == TPC:
                    then(nc.vector.tensor_scalar(var, mv[:, :, 1], EPS, None, ALU.add))
                    root.guess()
                elif part < TPC + 4:
                    root.improve()
                elif part == TPC + 4:
                    then(nc.vector.tensor_tensor(var2, rstd, rstd, ALU.mult))
                    then(nc.vector.tensor_tensor(var2, var2, mv[:, :, 1], ALU.mult))
                    then(nc.vector.tensor_scalar(var2, var2, EPS, None, ALU.add))
                elif part == TPC + 5:
                    root2.guess()
                elif part < TPC + 9:
                    root2.improve()
                elif part == TPC + 9:
                    then(nc.vector.tensor_tensor(rstd, rstd, rstd2, ALU.mult))
                    normed(n, 0)
                    normed(n, 1)

            def normed(n, j):
                t = TPC * n + j
                if t >= 2:
                    dve.wait_ge(transposed, t - 1)
                nc.vector.tensor_scalar(xn[:, j % 2, :], x[:, j, :], mv[:, j, 0:1], rstd[:, j:j + 1],
                                        ALU.subtract, ALU.mult).then_inc(xn_ready, 1)

            def z_lo(n, j):
                dve.wait_ge(zhi_ready, TPC * n + j + 1)
                cols = slice(j * P, (j + 1) * P)
                nc.vector.tensor_tensor(zt_lo[:, n % 2, :, cols], z[:, j % 2, :].rearrange("p (k t) -> p k t", k=KD),
                                        zt_hi[:, n % 2, :, cols], ALU.subtract).then_inc(zt_ready, 1)
                if j + 2 < TPC:
                    normed(n, j + 2)

            def update(u, g):
                ub = u % 2
                if g == 0:
                    dve.wait_ge(lv_done, L * u + 2)
                    dve.wait_ge(proj_used, 3 * u + 3)
                    for h in range(2):
                        hp = slice(h * HS, (h + 1) * HS)
                        last = nc.vector.tensor_tensor(r[hp, ub, h, :], r[hp, ub, h, :], decay[hp, ub, 0:TC], ALU.mult)
                    last.then_inc(updated, 1)
                    return
                m = LEVELS[g - 1]
                n = TC // (2 * m)
                dve.wait_ge(lv_done, L * u + g + 2)
                dve.wait_ge(updated, UPD * u + g)
                if g > 1:
                    dve.wait_ge(totalled, len(LEVELS) * u + g - 1)
                if g == UPD - 1 and u:
                    dve.wait_ge(y_done, u)
                total = decay[:, ub, OFF[g - 1]:OFF[g - 1] + TC // m].rearrange("p (n two) -> p n two", two=2)
                for h in range(2):
                    hp = slice(h * HS, (h + 1) * HS)
                    right = r[hp, ub, h, :].rearrange("p (n two m) -> p n two m", two=2, m=m)[:, :, 1, :]
                    new = right
                    if g == UPD - 1:
                        new = rsum[hp, :].rearrange("p (n two m) -> p n two m", two=2, m=m)[:, :, 1, :]
                    nc.vector.tensor_tensor(new, right, total[hp, :, 0:1].to_broadcast([HS, n, m]), ALU.mult)
                left = k[:, ub, :].rearrange("p (n two m) -> p n two m", two=2, m=m)[:, :, 0, :]
                nc.vector.tensor_tensor(left, left, total[:, :, 1:2].to_broadcast([P, n, m]), ALU.mult).then_inc(updated, 1)
                nc.vector.tensor_tensor(decay[:, ub, OFF[g]:OFF[g] + n], total[:, :, 0], total[:, :, 1],
                                        ALU.mult).then_inc(totalled, 1)

            def keep_scores(u, l):
                i, ub = L * u + l, u % 2
                dve.wait_ge(lv_done, i + 1)
                if l == 0 and u >= 2:
                    dve.wait_ge(y_done, u - 1)
                if l:
                    dve.wait_ge(kept_dve, ON_DVE * u + l)
                if l < 2:
                    out = mt[:, ub, 4 * l:4 * l + 4, :]
                    src = lv[i % 2][:, :].rearrange("p (g t) -> p g t", g=4)
                    mask = masks[:, 0:1, :].to_broadcast([P, 4, P])
                else:
                    m = LEVELS[l - 2]
                    nb = P // (2 * m)
                    out = mt[:, ub, :, :].rearrange("p g (n two m) -> p g n two m", two=2, m=m)[:, :, :, 1, :]
                    src = lv[i % 2][:, :].rearrange("p (g n m) -> p g n m", g=2 * Q, m=m)
                    mask = masks[:, l - 1, :].rearrange("p (n two m) -> p n two m", two=2, m=m)[:, :, 1, :]
                    mask = mask.unsqueeze(1).to_broadcast([P, 2 * Q, nb, m])
                nc.vector.copy_predicated(out, mask, src).then_inc(kept_dve, 1)

            def next_state(u, q):
                n, p, ub = u // NPAIR, u % NPAIR, u % 2
                if q == 0:
                    dve.wait_ge(kv_done, u + 1)
                    dve.wait_ge(totalled, len(LEVELS) * (u + 1))
                    if n >= B:
                        dve.wait_ge(carried, 2 * (u - B * NPAIR + 1))
                else:
                    dve.wait_ge(state_step, 2 * (Q - 1) * u + 2 * q)
                if q == Q - 1:
                    dve.wait_ge(y_done, u + 1)
                for h in range(2):
                    hp = slice(h * HS, (h + 1) * HS)
                    new = state[hp, ub, q, hp] if q < Q - 1 else carry[hp, n % B, p, hp]
                    old = state[hp, ub, q - 1, hp] if q else carry[hp, n % B, p, hp]
                    nc.vector.scalar_tensor_tensor(
                        out=new, in0=old, scalar=decay[hp, ub, OFF[-1] + q:OFF[-1] + q + 1],
                        in1=ks[hp, q * P + h * HS:q * P + (h + 1) * HS],
                        op0=ALU.mult, op1=ALU.add).then_inc(state_step if q < Q - 1 else carried, 1)

            def y_lo(u):
                dve.wait_ge(yhi_ready, u + 1)
                nc.vector.tensor_tensor(yt_lo[:, u % NPAIR, :], yb[:, :], yt_hi[:, u % NPAIR, :],
                                        ALU.subtract).then_inc(yt_ready, 1)

            def residual(n, j):
                t = TPC * n + j
                dve.wait_ge(out_done, t + 1)
                dve.wait_ge(res_loaded[j % 2], 16 * (t // 2 + 1))
                nc.vector.tensor_tensor(xres[:, j % 2, :], xres[:, j % 2, :], row[j % 2][:, :],
                                        ALU.add).then_inc(res_done, 1)

            for part in range(15):
                if part == TPC + 9:
                    norm(0, part)
                    for j in range(TPC):
                        z_lo(0, j)
                else:
                    norm(0, part)
            dve.wait_ge(consts_loaded, 16 * 5)
            nc.vector.tensor_scalar(neg_bw[:, :], bw[:, :], -1.0, None, ALU.mult).then_inc(negated, 1)
            dve.wait_ge(cleared, 3)
            dve.wait_ge(mt_cleared, 1)
            for u in range(NU + 1):
                for l in range(L):
                    if u < NU:
                        if l:
                            update(u, l - 1)
                        if l < ON_DVE:
                            keep_scores(u, l)
                    if u and l in (5, 6):
                        for q in (range(2), range(2, Q - 1))[l - 5]:
                            next_state(u - 1, q)
                    if u and l == 7:
                        y_lo(u - 1)
                    if u and l == 8:
                        next_state(u - 1, Q - 1)
                    for n, part in tiles_at(NORM_AT, u, l):
                        if n + 1 < NC:
                            norm(n + 1, part)
                    for n, j in tiles_at(T_AT, u, l):
                        if n + 1 < NC:
                            z_lo(n + 1, j)
                    for n, j in tiles_at(O_AT, u, l):
                        if n + 1 < NC:
                            residual(n, j)
            for j in range(TPC):
                residual(NC - 1, j)


def build(nc, x, w1g, w3g, w2t, wxt, ww, wk, wv, wr, wo, bw, gamma, beta, had, ident, masks, out):
    def scratch(name, shape, dt=F32):
        return nc.dram_tensor(name, shape, dt, kind="Internal").ap()
    w2p = scratch("w2p", [NG, P, HT, D])
    wxw = scratch("wxw", [P, KD, D])
    wo_hi = scratch("wo_hi", [P, KD, D])
    wo_lo = scratch("wo_lo", [P, KD, D])
    x1 = scratch("x1", [B * T, D])
    x2 = scratch("x2", [B * T, D])
    prepare_weights(nc, w2t, wxt, ww, wo, had, w2p, wxw, wo_hi, wo_lo)
    feed_forward(nc, "ffn1", x, x1, w1g, w3g, w2p, ident)
    mixing(nc, x1, x2, wr, wk, wv, wxw, wo_hi, wo_lo, gamma, beta, bw, ident, masks)
    feed_forward(nc, "ffn2", x2, out, w1g, w3g, w2p, ident)


def kernel(**inputs):
    import numpy as np
    import concourse.bacc as bacc
    from concourse.bass_utils import run_bass_kernel_spmd

    arr = {n: np.asarray(a) for n, a in inputs.items()}
    up = lambda w: np.ascontiguousarray(w.reshape(NG, GH, KD, P).transpose(0, 3, 2, 1))
    cols = lambda v: np.ascontiguousarray(v.reshape(KD, P).T)
    i = np.arange(P)
    bits = i[:, None] & i[None, :]
    odd = sum((bits >> n) & 1 for n in range(7)) & 1
    s, t = i[:, None], i[None, :]
    masks = [s == t] + [(s // (2 * m) == t // (2 * m)) & (s % (2 * m) < m) & (t % (2 * m) >= m) for m in LEVELS[:4]]
    data = {
        "x": arr["L0_attn_x"].reshape(B * T, D),
        "w1g": up(arr["L0_ffn_W1"]),
        "w3g": up(arr["L0_ffn_W3"]),
        "w2t": np.ascontiguousarray(arr["L0_ffn_W2"].T),
        "wxt": np.ascontiguousarray(arr["L0_attn_Wx"].T),
        "ww": arr["L0_attn_Ww"],
        "wk": arr["L0_attn_Wk"],
        "wv": arr["L0_attn_Wv"],
        "wr": arr["L0_attn_Wr"],
        "wo": arr["L0_attn_Wout"],
        "bw": cols(arr["L0_attn_bw"]),
        "gamma": cols(arr["L0_attn_gamma"]),
        "beta": cols(arr["L0_attn_beta"]),
        "had": np.stack([np.where(odd == 1, -1, 1), np.where(odd == 1, 1, -1)], 1).astype(np.float32),
        "ident": np.eye(P, dtype=np.float32),
        "masks": np.ascontiguousarray(np.stack(masks, 1).astype(np.int32)),
    }
    nc = bacc.Bacc("TRN2", target_bir_lowering=False, num_devices=1, dynamic_dma_scratch_size=1024)
    aps = {n: nc.dram_tensor(f"in_{n}", a.shape, mybir.dt.from_np(a.dtype), kind="ExternalInput").ap()
           for n, a in data.items()}
    out = nc.dram_tensor("out_x", (B * T, D), F32, kind="ExternalOutput").ap()
    build(nc, **aps, out=out)
    res = run_bass_kernel_spmd(nc, [{f"in_{n}": a for n, a in data.items()}], core_ids=[0])
    return res.results[0]["out_x"].reshape(B, T, D)
```

```python
import concourse.bass as bass
from concourse import mybir
from contextlib import ExitStack

F32 = mybir.dt.float32
F32R = mybir.dt.float32r
I32 = mybir.dt.int32
ALU = mybir.AluOpType
ACT = mybir.ActivationFunctionType

P = 128
B, T, D, H = 2, 1024, 512, 2048
NT = B * T // P
KD = D // P
TC = 512
NC = B * T // TC
TPC = TC // P
GH = 256
NG = H // GH
HT = GH // P
EPS = 1e-5
HS = 64
NPAIR = D // P
LEVELS = [1, 2, 4, 8, 16, 32, 64]
MAGIC = 0x5F3759DF


class Rsqrt:

    def __init__(self, nc, dve, step, count, v, y, t, half):
        self.nc, self.dve, self.step, self.count = nc, dve, step, count
        self.v, self.y, self.t, self.half = v, y, t, half

    def then(self, op):
        op.then_inc(self.step, 1)
        self.dve.wait_ge(self.step, self.count())

    def guess(self):
        vector = self.nc.vector
        self.then(vector.tensor_scalar(self.half, self.v, -0.5, None, ALU.mult))
        self.then(vector.tensor_scalar(self.t.bitcast(I32), self.v.bitcast(I32), 1, None, ALU.logical_shift_right))
        self.then(vector.tensor_scalar(self.y.bitcast(I32), self.t.bitcast(I32), -1.0, float(MAGIC), ALU.mult, ALU.add))

    def improve(self):
        vector = self.nc.vector
        self.then(vector.tensor_tensor(self.t, self.y, self.y, ALU.mult))
        self.then(vector.tensor_tensor(self.t, self.t, self.half, ALU.mult))
        self.then(vector.scalar_tensor_tensor(out=self.y, in0=self.t, scalar=1.5, in1=self.y, op0=ALU.add, op1=ALU.mult))


class Shared:

    def __init__(self, nc, ctx):
        def sb(name, shape, dt=F32):
            return ctx.enter_context(nc.sbuf_tensor(name, shape, dt))
        self.x0 = sb("x0", [P, TPC, D])
        self.raw = sb("raw", [P, 6, 2 * D])
        self.wb0 = sb("wb0", [P, 6, 2 * D], F32R)
        self.xt = sb("xt", [P, 3, 2, KD, TC], F32R)
        self.xn = sb("xn", [P, TPC, D])
        self.stored = [ctx.enter_context(nc.semaphore(f"stored{i}")) for i in range(2)]
        self.ident = sb("ident", [P, P])
        self.gamma = sb("gamma", [P, KD])
        self.beta = sb("beta", [P, KD])
        self.bw = sb("bw", [P, KD])
        self.stats = sb("stats", [P, TPC, 6])
        self.mv = sb("mv", [P, TPC, 2])
        small = sb("small", [P, 6, TPC])
        self.var, self.rstd, self.var2, self.rstd2, self.tmp, self.half = (small[:, i, :] for i in range(6))

    def group_raw(self, b):
        return [self.raw[:, 3 * b + m, :].rearrange("p (k c) -> p k c", c=GH if m < 2 else D) for m in range(3)]

    def group0_split(self):
        return [[self.wb0[:, 2 * m + i, :].rearrange("p (k c) -> p k c", c=GH if m < 2 else D) for i in range(2)]
                for m in range(3)]

    def third(self, t, i):
        return t[:, 2 * i:2 * i + 2, :].rearrange("p a (k d) -> p (a k) d", d=D)


class Norm:
    ONCE = TPC + 4
    TWICE = TPC + 10

    def __init__(self, nc, dve, step, count, sh):
        self.nc, self.sh = nc, sh
        self.root = Rsqrt(nc, dve, step, count, sh.var, sh.rstd, sh.tmp, sh.half)
        self.root2 = Rsqrt(nc, dve, step, count, sh.var2, sh.rstd2, sh.tmp, sh.half)

    def part(self, x, part):
        sh, vector, then = self.sh, self.nc.vector, self.root.then
        if part < TPC:
            then(vector.bn_stats(sh.stats[:, part, :], x[:, part, :]))
            then(vector.bn_aggr(sh.mv[:, part, :], sh.stats[:, part, :]))
        elif part == TPC:
            then(vector.tensor_scalar(sh.var, sh.mv[:, :, 1], EPS, None, ALU.add))
            self.root.guess()
        elif part < TPC + 4:
            self.root.improve()
        elif part == TPC + 4:
            then(vector.tensor_tensor(sh.var2, sh.rstd, sh.rstd, ALU.mult))
            then(vector.tensor_tensor(sh.var2, sh.var2, sh.mv[:, :, 1], ALU.mult))
            then(vector.tensor_scalar(sh.var2, sh.var2, EPS, None, ALU.add))
        elif part == TPC + 5:
            self.root2.guess()
        elif part < TPC + 9:
            self.root2.improve()
        elif part == TPC + 9:
            then(vector.tensor_tensor(sh.rstd, sh.rstd, sh.rstd2, ALU.mult))

    def normed(self, x, j):
        sh = self.sh
        return self.nc.vector.tensor_scalar(sh.xn[:, j, :], x[:, j, :], sh.mv[:, j, 0:1], sh.rstd[:, j:j + 1],
                                            ALU.subtract, ALU.mult)


def transposed_high(nc, act, xt, psum, j, transposed, count):
    act.wait_ge(transposed, count)
    return nc.scalar.activation(xt[:, 0, :, j * P:(j + 1) * P], psum[:, :].rearrange("p (k t) -> p k t", k=KD), ACT.Copy)


def transposed_low(nc, dve, xt, psum, j, hi_ready, count):
    dve.wait_ge(hi_ready, count)
    cols = slice(j * P, (j + 1) * P)
    return nc.vector.tensor_tensor(xt[:, 1, :, cols], psum[:, :].rearrange("p (k t) -> p k t", k=KD),
                                   xt[:, 0, :, cols], ALU.subtract)


def prepare_weights(nc, sh, x, w1g, w3g, w2t, wxt, ww, had, ident, gamma, beta, bw, w2p, wxw):
    NB = H // P
    STAGES = 3
    DQ = D // 4
    QT = 4
    with ExitStack() as ctx:
        def sb(name, shape, dt=F32):
            return ctx.enter_context(nc.sbuf_tensor(name, shape, dt))

        def sem(name):
            return ctx.enter_context(nc.semaphore(name))
        fly = sb("fly", [P, 4, NB, DQ])
        other = sb("other", [P, 2, NB, DQ])
        other_hi, other_lo = (sh.xt[:, i].rearrange("p q k t -> p q (k t)").rearrange("p q (b d) -> p q b d", d=DQ)
                              for i in (1, 2))
        had_sb = sb("had_sb", [P, 2, P])
        had_r = sb("had_r", [P, 2, P], F32R)
        wx_sb = sb("wx_sb", [P, KD, D])
        ww_sb = sb("ww_sb", [P, KD, D])
        wxw_sb = sb("wxw_sb", [P, KD, D])
        ps = [ctx.enter_context(nc.psum_tensor(f"prep_ps{i}", [P, D], F32)) for i in range(4)]
        ps_w = [ctx.enter_context(nc.psum_tensor(f"prep_ps_w{i}", [P, D], F32)) for i in range(2)]
        w2_loaded = [sem(f"w2_loaded{q}") for q in range(4)]
        had_loaded = sem("had_loaded")
        wx_loaded = sem("wx_loaded")
        x_loaded = sem("prep_x_loaded")
        consts_loaded = sem("consts_loaded")
        group_loaded = [sem(f"group_loaded{m}") for m in range(2)]
        had_ready = sem("had_ready")
        flown = sem("flown")
        other_hi_ready = sem("other_hi_ready")
        other_lo_ready = sem("other_lo_ready")
        last_lo_ready = sem("last_lo_ready")
        transposed = sem("prep_transposed")
        xt_hi_ready = sem("prep_xt_hi_ready")
        xt_ready = sem("prep_xt_ready")
        prod = sem("prod")
        prod_w = sem("prod_w")
        copied = sem("copied")
        copied_w = sem("copied_w")
        w2_stored = sem("w2_stored")
        hi_ready = sem("prep_hi_ready")
        lo_ready = sem("prep_lo_ready")
        wxw_stored = sem("wxw_stored")
        ln_step = sem("prep_ln_step")
        xn_ready = sem("prep_xn_ready")
        block = ctx.enter_context(nc.Block())
        splits = [(raw, hi, lo) for raw, (hi, lo) in zip(sh.group_raw(0)[:2], sh.group0_split()[:2])]

        @block.sync
        def _(sp):
            w2_v = w2t.rearrange("(b p) d -> p b d", p=P)
            w2p_v = w2p.rearrange("g p h d -> p g h d")

            def load(dst, src, signal):
                sp.dma_start(dst, src).then_inc(signal, 16)

            def load_w2(q):
                load(fly[:, q, :, :], w2_v[:, :, q * DQ:(q + 1) * DQ], w2_loaded[q])
            load_w2(0)
            load(had_sb[:, :, :], had, had_loaded)
            load_w2(1)
            load(wx_sb[:, :, :], wxt.rearrange("(k p) d -> p k d", p=P), wx_loaded)
            load(ww_sb[:, :, :], ww.rearrange("(k p) d -> p k d", p=P), wx_loaded)
            load_w2(2)
            load_w2(3)
            load(sh.x0[:, :, :], x.rearrange("(c n p) d -> c p n d", p=P, n=TPC)[0], x_loaded)
            for m, src in enumerate((w1g, w3g)):
                load(sh.group_raw(0)[m], src[0], group_loaded[m])
            for dst, src in ((sh.ident, ident), (sh.gamma, gamma), (sh.beta, beta), (sh.bw, bw)):
                load(dst[:, :], src, consts_loaded)
            for q in range(4):
                if q == 3:
                    sp.wait_ge(copied_w, KD)
                    sp.dma_start(wxw, wxw_sb[:, :, :]).then_inc(wxw_stored, 16)
                sp.wait_ge(copied, 4 * (q + 1))
                for h in range(HT):
                    sp.dma_start(w2p_v[:, :, h, q * DQ:(q + 1) * DQ],
                                 fly[:, q, :, :].rearrange("p (g h) d -> p g h d", h=HT)[:, :, h, :]
                                 ).then_inc(w2_stored, 16)
            sp.wait_ge(w2_stored, 16 * HT * 4)
            sp.wait_ge(wxw_stored, 16)
            sp.wait_ge(consts_loaded, 16 * 4)

        @block.vector
        def _(dve):
            steps = [0]

            def count():
                steps[0] += 1
                return steps[0]
            for q in range(4):
                dve.wait_ge(w2_loaded[q], 16)
                if q >= 2:
                    dve.wait_ge(other_lo_ready, q - 1)
                pair = (fly[:, q], other[:, q % 2])
                for s in range(STAGES):
                    if s:
                        dve.wait_ge(flown, 2 * STAGES * q + 2 * s)
                    src, dst = (pair[(s + i) % 2].rearrange("p (n two h) d -> p n two (h d)", two=2, h=1 << s)
                                for i in range(2))
                    nc.vector.tensor_tensor(dst[:, :, 0], src[:, :, 0], src[:, :, 1], ALU.add).then_inc(flown, 1)
                    nc.vector.tensor_tensor(dst[:, :, 1], src[:, :, 0], src[:, :, 1], ALU.subtract).then_inc(flown, 1)
            dve.wait_ge(other_hi_ready, 4)
            nc.vector.tensor_tensor(other_lo[:, 1], other[:, 1], other_hi[:, 1], ALU.subtract).then_inc(last_lo_ready, 1)
            norm = Norm(nc, dve, ln_step, count, sh)
            dve.wait_ge(x_loaded, 16)
            for part in range(Norm.ONCE):
                norm.part(sh.x0, part)
            for j in range(TPC):
                norm.normed(sh.x0, j).then_inc(xn_ready, 1)
            for j in range(TPC):
                transposed_low(nc, dve, sh.xt[:, 0], ps_w[j % 2], j, xt_hi_ready, j + 1).then_inc(xt_ready, 1)

        @block.gpsimd
        def _(pool):
            def split_lo(n):
                raw, hi, lo = splits[n]
                pool.wait_ge(hi_ready, n + 1)
                nc.gpsimd.tensor_tensor(lo, raw, hi, ALU.subtract).then_inc(lo_ready, 1)
            for q in range(3):
                pool.wait_ge(other_hi_ready, q + 1)
                nc.gpsimd.tensor_tensor(other_lo[:, q % 2], other[:, q % 2], other_hi[:, q % 2],
                                        ALU.subtract).then_inc(other_lo_ready, 1)
            split_lo(0)
            split_lo(1)

        @block.tensor
        def _(pe):
            def transform(q):
                for part in range(4):
                    if q:
                        pe.wait_ge(copied, 4 * (q - 1) + part + 1)
                    low = QT * (part % 2)
                    halves = [(slice(low + half * NB // 2, low + half * NB // 2 + QT), 1 if part >= 2 and half else 0)
                              for half in range(2)]
                    for n, term in enumerate((other_hi, other_lo)):
                        if n and part == 0:
                            if q < 3:
                                pe.wait_ge(other_lo_ready, q + 1)
                            else:
                                pe.wait_ge(last_lo_ready, 1)
                        for tiles, sign in halves:
                            last = nc.tensor.matmul(ps[part][:, :], had_r[:, sign, :], term[:, q % 2, tiles, :],
                                                    start=(n == 0 and tiles.start == low),
                                                    stop=(n == 1 and tiles.start > low))
                    last.then_inc(prod, 1)

            def small_product(m):
                if m == 0:
                    pe.wait_ge(wx_loaded, 32)
                if m >= 2:
                    pe.wait_ge(copied_w, m - 1)
                for k in range(KD):
                    last = nc.tensor.matmul(ps_w[m % 2][:, :], wx_sb[:, k, m * P:(m + 1) * P], ww_sb[:, k, :],
                                            start=(k == 0), stop=(k == KD - 1))
                last.then_inc(prod_w, 1)

            pe.wait_ge(had_ready, 1)
            for q in range(4):
                small_product(q)
                pe.wait_ge(other_hi_ready, q + 1)
                transform(q)
            pe.wait_ge(consts_loaded, 16 * 4)
            for j in range(TPC):
                pe.wait_ge(xn_ready, j + 1)
                if j < 2:
                    pe.wait_ge(copied_w, 3 + j)
                else:
                    pe.wait_ge(xt_ready, j - 1)
                for k in range(KD):
                    cols = slice(k * P, (k + 1) * P)
                    last = nc.tensor.transpose(ps_w[j % 2][:, cols], sh.xn[:, j, cols], sh.ident[:, :])
                last.then_inc(transposed, 1)

        @block.scalar
        def _(act):
            def split_hi(n):
                act.wait_ge(group_loaded[n], 16)
                nc.scalar.activation(splits[n][1], splits[n][0], ACT.Copy).then_inc(hi_ready, 1)

            def other_high(q):
                act.wait_ge(flown, 2 * STAGES * (q + 1))
                if q >= 2:
                    act.wait_ge(prod, 4 * (q - 1))
                nc.scalar.activation(other_hi[:, q % 2], other[:, q % 2], ACT.Copy).then_inc(other_hi_ready, 1)
            act.wait_ge(had_loaded, 16)
            nc.scalar.activation(had_r[:, :, :], had_sb[:, :, :], ACT.Copy).then_inc(had_ready, 1)
            def small_copy(m):
                act.wait_ge(prod_w, m + 1)
                nc.scalar.activation(wxw_sb[:, m, :], ps_w[m % 2][:, :], ACT.Copy).then_inc(copied_w, 1)
            other_high(0)
            other_high(1)
            for q in range(4):
                small_copy(q)
                if q in (1, 2):
                    other_high(q + 1)
                if q == 3:
                    split_hi(0)
                    split_hi(1)
                for part in range(4):
                    act.wait_ge(prod, 4 * q + part + 1)
                    nc.scalar.activation(fly[:, q, QT * part:QT * part + QT, :], ps[part][:, :], ACT.Copy,
                                         scale=0.5 / H ** 0.5).then_inc(copied, 1)
            for j in range(TPC):
                transposed_high(nc, act, sh.xt[:, 0], ps_w[j % 2], j, transposed, j + 1).then_inc(xt_hi_ready, 1)


def feed_forward(nc, sh, tag, x_in, x_out, w1g, w3g, w2p, in_stored, stored, mix_weights):
    with ExitStack() as ctx:
        def sb(name, shape, dt=F32):
            return ctx.enter_context(nc.sbuf_tensor(f"{tag}_{name}", shape, dt))

        def sem(name):
            return ctx.enter_context(nc.semaphore(f"{tag}_{name}"))
        x_rest = sb("x_rest", [P, NC - 1, TPC, D])
        x = [sh.x0] + [x_rest[:, c] for c in range(NC - 1)]
        xt_last = sb("xt_last", [P, 2, KD, TC], F32R)
        xt = [sh.xt[:, c] for c in range(NC - 1)] + [xt_last]
        xt_hi, xt_lo = ([chunk[:, i] for chunk in xt] for i in range(2))
        wb1 = sb("wb1", [P, 6, 2 * D], F32R)
        w_odd = [[wb1[:, 2 * m + i, :].rearrange("p (k c) -> p k c", c=GH if m < 2 else D) for i in range(2)]
                 for m in range(3)]
        raw = [sh.group_raw(b) for b in range(2)]
        w_hi, w_lo = ([[parts[i] for parts in split] for split in (sh.group0_split(), w_odd)] for i in range(2))
        silu = sb("silu", [P, 2, TC])
        hid = sb("hid", [P, 2, TC])
        hid_hi = sb("hid_hi", [P, 2, HT, TC], F32R)
        hid_lo = sb("hid_lo", [P, 2, HT, TC], F32R)
        xn, ident = sh.xn, sh.ident
        if mix_weights:
            mix_raw = [sh.third(sh.raw, i) for i in (0, 2, 1, 0)]
            mix_split = [[sh.xt[:, c, i] for i in range(2)] for c in range(3)]
            mix_split += [[sh.third(sh.wb0, i) for i in range(2)]]

        def bank(name):
            return ctx.enter_context(nc.psum_tensor(f"{tag}_{name}", [P, TC], F32))
        gate = [bank(f"gate{i}") for i in range(HT)]
        lin = [bank(f"lin{i}") for i in range(HT)]
        down = [bank(f"down{i}") for i in range(TPC)]

        x_loaded = {c: sem(f"x_loaded{c}") for c in range(2, NC)}
        x1_loaded = [sem(f"x1_loaded{j}") for j in range(TPC)]
        mix_loaded = [sem(f"mix_loaded{n}") for n in range(4)]
        mix_hi = sem("mix_hi")
        mix_lo = sem("mix_lo")
        raw_loaded = [[sem(f"raw{m}_loaded{b}") for b in range(2)] for m in (1, 3, 2)]
        weights_hi = sem("weights_hi")
        weights_lo = sem("weights_lo")
        ln_step = sem("ln_step")
        xn_ready = sem("xn_ready")
        transposed = sem("transposed")
        xt_hi_ready = sem("xt_hi_ready")
        xt_ready = sem("xt_ready")
        gate_done = sem("gate_done")
        lin_done = sem("lin_done")
        silu_done = sem("silu_done")
        hid_done = sem("hid_done")
        hi_done = sem("hi_done")
        lo_done = sem("lo_done")
        down_done = sem("down_done")
        added = sem("added")
        stored = stored or sem("stored")
        block = ctx.enter_context(nc.Block())
        STEPS = NG * NC
        PER = 2 * NC

        xin_v = x_in.rearrange("(c n p) d -> c p n d", p=P, n=TPC)
        xout_v = x_out.rearrange("(n p) d -> p n d", p=P)

        def parts_split(g3):
            return g3 - 2

        @block.sync
        def _(sp):
            def load_part(g, b, m):
                sp.dma_start(raw[b][m], (w1g, w3g, w2p)[m][g]).then_inc(raw_loaded[m][b], 16)

            def load_x(c):
                sp.dma_start(x[c], xin_v[c]).then_inc(x_loaded[c], 16)

            def load_mix(n):
                sp.dma_start(mix_raw[n], mix_weights[n]).then_inc(mix_loaded[n], 16)
            for j in range(TPC):
                sp.dma_start(x[1][:, j, :], xin_v[1][:, j, :]).then_inc(x1_loaded[j], 16)
            load_part(0, 0, 2)
            if in_stored:
                sp.wait_ge(*in_stored)
            load_x(2)
            load_x(3)
            for m in range(3):
                load_part(1, 1, m)
            with sp.Fori(1, NG // 2) as i:
                for b in range(2):
                    sp.wait_ge(weights_lo, parts_split(6 * i + 3 * b - 3))
                    for m in range(3):
                        load_part(2 * i + b, b, m)
            if mix_weights:
                sp.wait_ge(weights_lo, parts_split(3 * NG))
                for n in range(3):
                    load_mix(n)
            for t in range(NT):
                sp.wait_ge(added, (STEPS - NC) * TPC + t + 1)
                sp.dma_start(xout_v[:, t, :], x[t // TPC][:, t % TPC, :]).then_inc(stored, 16)
                if mix_weights and t == TPC - 1:
                    sp.wait_ge(mix_lo, 1)
                    load_mix(3)
            if not mix_weights:
                sp.wait_ge(stored, 16 * NT)

        @block.gpsimd
        def _(pool):
            def low_parts(g3, b, first=0):
                for m in range(first, 3):
                    pool.wait_ge(weights_hi, parts_split(g3 + m + 1))
                    nc.gpsimd.tensor_tensor(w_lo[b][m], raw[b][m], w_hi[b][m], ALU.subtract).then_inc(weights_lo, 1)
            low_parts(0, 0, 2)
            low_parts(3, 1)
            with pool.Fori(1, NG // 2) as i:
                for b in range(2):
                    low_parts(6 * i + 3 * b, b)
            if mix_weights:
                for n in range(4):
                    pool.wait_ge(mix_hi, n + 1)
                    nc.gpsimd.tensor_tensor(mix_split[n][1], mix_raw[n], mix_split[n][0], ALU.subtract).then_inc(mix_lo, 1)

        @block.tensor
        def _(pe):
            def transposes(c, free):
                for j in range(TPC):
                    t = c * TPC + j
                    pe.wait_ge(xn_ready, t - TPC + 1)
                    free(j)
                    for k in range(KD):
                        cols = slice(k * P, (k + 1) * P)
                        last = nc.tensor.transpose(down[j][:, cols], xn[:, j, cols], ident[:, :])
                    last.then_inc(transposed, 1)

            def up(n, j, h, group3, between=None):
                b, c = (j // NC) % 2, j % NC
                cols = slice(h * P, (h + 1) * P)
                for m, (psum, done, used) in enumerate(((gate[h], gate_done, silu_done), (lin[h], lin_done, hid_done))):
                    if m and between:
                        between()
                    hi, lo = w_hi[b][m], w_lo[b][m]
                    if c == 0 and h == 0 and not (isinstance(n, int) and n == 0):
                        pe.wait_ge(weights_lo, parts_split(group3 + m + 1))
                    if not (isinstance(n, int) and n == 0):
                        pe.wait_ge(used, HT * n + h - 1)
                    for k in range(KD):
                        nc.tensor.matmul(psum[:, :], hi[:, k, cols], xt_hi[c][:, k, :], start=(k == 0), stop=False)
                        nc.tensor.matmul(psum[:, :], hi[:, k, cols], xt_lo[c][:, k, :], start=False, stop=False)
                        last = nc.tensor.matmul(psum[:, :], lo[:, k, cols], xt_hi[c][:, k, :],
                                                start=False, stop=(k == KD - 1))
                    last.then_inc(done, 1)

            def downs(n, j, group3, free):
                b, s = (j // NC) % 2, j % 2
                hi, lo = w_hi[b][2], w_lo[b][2]
                if j % NC == 0:
                    pe.wait_ge(weights_lo, parts_split(group3 + 3))
                pe.wait_ge(lo_done, HT * n + HT)
                for t in range(TPC):
                    free(t)
                    cols = slice(t * P, (t + 1) * P)
                    for h in range(HT):
                        nc.tensor.matmul(down[t][:, :], hid_hi[:, s, h, cols], hi[:, h, :], start=(h == 0), stop=False)
                        nc.tensor.matmul(down[t][:, :], hid_hi[:, s, h, cols], lo[:, h, :], start=False, stop=False)
                        last = nc.tensor.matmul(down[t][:, :], hid_lo[:, s, h, cols], hi[:, h, :],
                                                start=False, stop=(h == HT - 1))
                    last.then_inc(down_done, 1)

            def banks_added(n):
                return lambda t: pe.wait_ge(added, TPC * n - TPC + t + 1)

            def lo_written(c):
                return lambda t: pe.wait_ge(xt_ready, TPC * (c - 1) + t + 1)

            for n in range(PER):
                g3 = 3 * (n // NC)
                if 1 <= n < NC:
                    pe.wait_ge(xt_ready, TPC * n)
                up(n, n, 0, g3)
                up(n, n, 1, g3, None if n else lambda: transposes(1, lambda j: None))
                if 1 <= n < NC - 1:
                    transposes(n + 1, lo_written(1) if n == 1 else lambda j: pe.wait_ge(added, TPC * (n - 2) + j + 1))
                if n:
                    downs(n - 1, n - 1, 3 * ((n - 1) // NC), lo_written(n + 1) if n + 1 < NC else
                          lo_written(NC - 1) if n < 3 else banks_added(n - 1))
            with pe.Fori(1, NG // 2) as i:
                for j in range(PER):
                    for h in range(HT):
                        up(PER * i + j, j, h, 6 * i + 3 * (j // NC))
                    downs(PER * i + (j - 1), (j - 1) % PER, 6 * i + (3 * ((j - 1) // NC) if j else -3),
                          banks_added(PER * i + (j - 1)))
            downs(STEPS - 1, PER - 1, 3 * (NG - 1), banks_added(STEPS - 1))

        @block.scalar
        def _(act):
            def transposed_hi(c):
                for j in range(TPC):
                    transposed_high(nc, act, xt[c], down[j], j, transposed, TPC * (c - 1) + j + 1).then_inc(xt_hi_ready, 1)

            def hidden_tile(n, j, h):
                act.wait_ge(gate_done, HT * n + h + 1)
                if not (isinstance(n, int) and n == 0):
                    act.wait_ge(hid_done, HT * n + h - 1)
                nc.scalar.activation(silu[:, h, :], gate[h][:, :], ACT.Silu).then_inc(silu_done, 1)
                act.wait_ge(hid_done, HT * n + h + 1)
                if not (isinstance(n, int) and n < 2):
                    act.wait_ge(down_done, TPC * n - TPC)
                nc.scalar.activation(hid_hi[:, j % 2, h, :], hid[:, h, :], ACT.Copy).then_inc(hi_done, 1)

            def hidden(n, j):
                for h in range(HT):
                    hidden_tile(n, j, h)

            def high_parts(b, loads, free, first=0):
                if free is not None:
                    act.wait_ge(down_done, free)
                for m in range(first, 3):
                    act.wait_ge(raw_loaded[m][b], loads - 16 if b == 0 and m < 2 else loads)
                    nc.scalar.activation(w_hi[b][m], raw[b][m], ACT.Copy).then_inc(weights_hi, 1)

            def mix_high(n):
                act.wait_ge(mix_loaded[n], 16)
                if n < 3:
                    act.wait_ge(lin_done, HT * (STEPS - NC + n + 1))
                    act.wait_ge(gate_done, HT * (STEPS - NC + n + 1))
                nc.scalar.activation(mix_split[n][0], mix_raw[n], ACT.Copy).then_inc(mix_hi, 1)

            def turn(i):
                last = isinstance(i, int) and i == NG // 2 - 1
                for j in range(PER):
                    if j > NC and last and mix_weights:
                        mix_high(j - NC - 1)
                        if j == PER - 1:
                            mix_high(3)
                    hidden(PER * i + j, j)
                    if j == 1:
                        high_parts(1, 16 * i + 16, (2 * i) * NC * TPC)
                    if j == NC + 1 and not last:
                        high_parts(0, 16 * i + 32, (2 * i + 1) * NC * TPC)

            high_parts(0, 16, None, 2)
            transposed_hi(1)
            for n in range(PER):
                hidden_tile(n, n, 0)
                if 1 <= n < NC - 1:
                    transposed_hi(n + 1)
                hidden_tile(n, n, 1)
                if n == 1:
                    high_parts(1, 16, None)
                if n == NC + 1:
                    high_parts(0, 32, NC * TPC)
            with act.Fori(1, NG // 2 - 1) as i:
                turn(i)
            turn(NG // 2 - 1)

        @block.vector
        def _(dve):
            steps = [0]

            def count():
                steps[0] += 1
                return steps[0]

            norm = Norm(nc, dve, ln_step, count, sh)

            def normed(c):
                if c > 1:
                    dve.wait_ge(x_loaded[c], 16)
                for part in range(Norm.ONCE):
                    if c == 1 and part < TPC:
                        dve.wait_ge(x1_loaded[part], 16)
                    norm.part(x[c], part)
                for j in range(TPC):
                    if c > 1:
                        dve.wait_ge(transposed, TPC * (c - 2) + j + 1)
                    norm.normed(x[c], j).then_inc(xn_ready, 1)

            def transposed_lo(c):
                for j in range(TPC):
                    transposed_low(nc, dve, xt[c], down[j], j, xt_hi_ready, TPC * (c - 1) + j + 1).then_inc(xt_ready, 1)

            def hidden_tile(n, j, h):
                dve.wait_ge(silu_done, HT * n + h + 1)
                dve.wait_ge(lin_done, HT * n + h + 1)
                if not (isinstance(n, int) and n == 0):
                    dve.wait_ge(lo_done, HT * n + h - 1)
                nc.vector.tensor_tensor(hid[:, h, :], silu[:, h, :], lin[h][:, :], ALU.mult).then_inc(hid_done, 1)
                dve.wait_ge(hi_done, HT * n + h + 1)
                nc.vector.tensor_tensor(hid_lo[:, j % 2, h, :], hid[:, h, :], hid_hi[:, j % 2, h, :],
                                        ALU.subtract).then_inc(lo_done, 1)

            def hidden(n, j):
                for h in range(HT):
                    hidden_tile(n, j, h)

            def add(n, j, before):
                c = j % NC
                for t in range(TPC):
                    dve.wait_ge(down_done, TPC * n + t + 1)
                    if before:
                        dve.wait_ge(added, TPC * n - NC * TPC + t + 1)
                    xt = x[c][:, t, :]
                    nc.vector.tensor_tensor(xt, xt, down[t][:, :], ALU.add).then_inc(added, 1)
            normed(1)
            transposed_lo(1)
            for n in range(PER):
                hidden_tile(n, n, 0)
                if 1 <= n < NC - 1:
                    transposed_lo(n + 1)
                hidden_tile(n, n, 1)
                if n + 2 < NC:
                    normed(n + 2)
                if n >= 1:
                    add(n - 1, n - 1, n - 1 >= NC)

            def turn(i):
                for j in range(PER):
                    hidden(PER * i + j, j)
                    add(PER * i + (j - 1), (j - 1) % PER, True)
                    if isinstance(i, int) and mix_weights and NC + 1 <= j < NC + 3:
                        half = j - NC - 1
                        if half == 0:
                            dve.wait_ge(added, (STEPS - NC + 1) * TPC)
                        for part in range(half * Norm.TWICE // 2, (half + 1) * Norm.TWICE // 2):
                            norm.part(x[0], part)
                        if half:
                            for t in range(2):
                                norm.normed(x[0], t).then_inc(xn_ready, 1)
            with dve.Fori(1, NG // 2 - 1) as i:
                turn(i)
            turn(NG // 2 - 1)
            add(STEPS - 1, PER - 1, True)


def mixing(nc, sh, x_in, x_out, w1g, w3g, wo_in, masks_in, in_stored, last_stored):
    NU = NC * NPAIR
    CPB = T // TC
    Q = TC // P
    L = 2 + len(LEVELS)
    UPD = 1 + len(LEVELS)
    ON_DVE = 6
    ON_ACT = L - ON_DVE
    OFF = [2 * TC - (2 * TC >> i) for i in range(len(LEVELS) + 1)]
    SPC = NPAIR
    NORM_PARTS = Norm.TWICE
    NORM_AT = {(u, l): L * u + l for u in range(2) for l in range(L) if L * u + l < NORM_PARTS}
    T_AT = {(2, 0): 0, (2, 2): 1, (2, 3): 2, (2, 5): 3}
    XN_AT = {(2, 1): 2, (2, 3): 3}
    V_AT = {(2, 8): 0, (3, 0): 1, (3, 2): 2, (3, 5): 3, (3, 7): 4, (4, 0): 5, (4, 2): 6, (4, 5): 7}
    O_AT = {(5, i): i for i in range(8)}
    V0_AT = {(0, 2 * i + 1): TPC + i for i in range(TPC)}
    O_LATE = {(NC * NPAIR - 1, i): i for i in range(8)}

    def tiles_at(table, u, l):
        for (du, dl), j in table.items():
            if dl == l and (u - du) % SPC == 0 and 0 <= (u - du) // SPC < NC:
                yield (u - du) // SPC, j

    def out_at(u, l):
        for n, i in tiles_at(O_AT, u, l):
            if n < NC - 2:
                yield n, i
        if (u, l) in O_LATE:
            yield NC - 2, O_LATE[u, l]

    with ExitStack() as ctx:
        def sb(name, shape, dt=F32):
            return ctx.enter_context(nc.sbuf_tensor(f"mix_{name}", shape, dt))

        def sem(name):
            return ctx.enter_context(nc.semaphore(f"mix_{name}"))
        WR, WK, WXW, WV, WO = range(5)
        wo_split = sb("wo_split", [P, 2, KD, D], F32R)
        w_hi, w_lo = ([sh.xt[:, c, i] for c in range(3)] + [sh.third(sh.wb0, i), wo_split[:, i]] for i in range(2))
        x = sh.x0
        xres = sb("xres", [P, 2, D])
        xn, z = sh.xn[:, 0:2], sh.xn[:, 2:4]
        zt_rest = sb("zt_rest", [P, 3, KD, TC], F32R)
        zt_hi = [sh.third(sh.wb0, 2), zt_rest[:, 0]]
        zt_lo = [zt_rest[:, 1], zt_rest[:, 2]]
        v = [sh.third(sh.raw, 0), sh.third(sh.raw, 2)]
        group0 = [(raw, hi, lo) for raw, (hi, lo) in zip(sh.group_raw(0)[:2], sh.group0_split()[:2])]
        r = sb("r", [P, 2, 2, TC])
        k = sb("k", [P, 2, TC])
        decay = sh.raw[:, 2:4, :]
        rsum = sb("rsum", [P, TC])
        mt = sb("mt", [P, 2, 2 * Q, P])
        ktok = sb("ktok", [P, TC])
        state = sb("state", [P, 2, Q - 1, P])
        carry = sb("carry", [P, B, NPAIR, P])
        yt_hi = sb("yt_hi", [P, NPAIR, TC], F32R)
        yt_lo = sb("yt_lo", [P, NPAIR, TC], F32R)
        y_t = [(yt_hi, yt_lo)] * (NC - 1) + [(zt_hi[NC % 2], zt_lo[NC % 2])]
        masks = sb("masks", [P, ON_DVE - 1, P], I32)
        neg_bw = sb("neg_bw", [P, KD])
        ident, gamma, beta = sh.ident, sh.gamma, sh.beta

        def bank(name):
            return ctx.enter_context(nc.psum_tensor(f"mix_{name}", [P, TC], F32))
        row = [bank(f"row{i}") for i in range(2)]
        pj = [bank(f"pj{i}") for i in range(2)]
        lv = [bank(f"lv{i}") for i in range(2)]
        yb = bank("yb")
        ks = bank("ks")
        last_out = row + pj

        def residual_tile(n, j):
            return r[:, (NU - 2) % 2, j - 2, :] if n == NC - 1 and j >= 2 else xres[:, j % 2, :]

        masks_loaded = sem("masks_loaded")
        wo_loaded = sem("wo_loaded")
        wo_hi_ready = sem("wo_hi_ready")
        wo_ready = sem("wo_ready")
        next_x_loaded = sem("next_x_loaded")
        group_loaded = [sem(f"group_loaded{m}") for m in range(2)]
        group_hi = sem("group_hi")
        group_lo = sem("group_lo")
        next_xn_ready = sem("next_xn_ready")
        next_transposed = sem("next_transposed")
        next_hi_ready = sem("next_hi_ready")
        next_xt_ready = sem("next_xt_ready")
        x_loaded = sem("x_loaded")
        res_loaded = [sem(f"res_loaded{i}") for i in range(2)]
        last_res_loaded = sem("last_res_loaded")
        x_stored = [sem(f"x_stored{i}") for i in range(2)]
        cleared = sem("cleared")
        negated = sem("negated")
        ln_step = sem("ln_step")
        xn_ready = sem("xn_ready")
        transposed = sem("transposed")
        z_ready = sem("z_ready")
        zhi_ready = sem("zhi_ready")
        zt_ready = sem("zt_ready")
        v_done = sem("v_done")
        v_ready = sem("v_ready")
        proj_done = sem("proj_done")
        proj_used = sem("proj_used")
        lv_done = sem("lv_done")
        kept_dve = sem("kept_dve")
        kept_act = sem("kept_act")
        updated = sem("updated")
        k_updated = sem("k_updated")
        totalled = sem("totalled")
        rsum_left = sem("rsum_left")
        kt_done = sem("kt_done")
        ktok_ready = sem("ktok_ready")
        kv_done = sem("kv_done")
        state_step = sem("state_step")
        carried = sem("carried")
        y_done = sem("y_done")
        yhi_ready = sem("yhi_ready")
        yt_ready = sem("yt_ready")
        out_done = sem("out_done")
        res_done = sem("res_done")
        block = ctx.enter_context(nc.Block())

        xin_v = x_in.rearrange("(b c n p) d -> b c p n d", b=B, c=CPB, p=P)
        xout_v = x_out.rearrange("(b c n p) d -> b c n p d", b=B, c=CPB, p=P)

        def v_bank(n, j):
            return (row if n else (ks, yb))[j % 2]

        def normed_here(tiles):
            return tiles - 2


        @block.sync
        def _(sp):
            def load_x(n):
                sp.dma_start(x[:, :, :], xin_v[n % B, n // B]).then_inc(x_loaded, 16)

            def load_res(n, j):
                sp.dma_start(xres[:, j % 2, :], xin_v[n % B, n // B][:, j, :]).then_inc(res_loaded[j % 2], 16)
            sp.dma_start(masks[:, :, :], masks_in).then_inc(masks_loaded, 16)
            sp.wait_ge(*in_stored)
            for i in range(2):
                if i:
                    sp.wait_ge(wo_ready, i)
                sp.dma_start(xres[:, :, :], wo_in[:, 2 * i:2 * i + 2, :]).then_inc(wo_loaded, 16)
            sp.wait_ge(wo_ready, 2)
            load_res(0, 0)
            load_res(0, 1)
            sp.wait_ge(xn_ready, normed_here(TPC))
            load_x(1)
            for n in range(NC):
                if n + 2 < NC:
                    sp.wait_ge(xn_ready, normed_here(TPC * (n + 2)))
                    load_x(n + 2)
                if n == NC - 2:
                    sp.wait_ge(xn_ready, normed_here(NT))
                    sp.dma_start(x[:, :, :], xout_v[0, 0].rearrange("n p d -> p n d")).then_inc(next_x_loaded, 16)
                    sp.wait_ge(y_done, NPAIR * (NC - 1))
                    for m, src in enumerate((w1g, w3g)):
                        sp.dma_start(group0[m][0], src[0]).then_inc(group_loaded[m], 16)
                if n == NC - 1:
                    sp.wait_ge(lv_done, L * (NU - 1))
                    sp.wait_ge(updated, UPD * (NU - 1))
                    sp.wait_ge(rsum_left, NU - 1)
                    for j in range(2, TPC):
                        sp.dma_start(residual_tile(n, j), xin_v[n % B, n // B][:, j, :]).then_inc(last_res_loaded, 16)
                for j in range(TPC):
                    t = TPC * n + j
                    sp.wait_ge(res_done, t + 1)
                    out = xout_v[n % B, n // B, j]
                    if n == NC - 1:
                        sp.dma_start(out, residual_tile(n, j)).then_inc(last_stored, 16)
                    else:
                        sp.dma_start(out, residual_tile(n, j)).then_inc(x_stored[j % 2], 16)
                        sp.wait_ge(x_stored[j % 2], 16 * (t // 2 + 1))
                        load_res((t + 2) // TPC, (t + 2) % TPC)

        @block.gpsimd
        def _(pool):
            def z_lo(n, j):
                pool.wait_ge(zhi_ready, TPC * n + j + 1)
                cols = slice(j * P, (j + 1) * P)
                nc.gpsimd.tensor_tensor(zt_lo[n % 2][:, :, cols], z[:, j % 2, :].rearrange("p (k t) -> p k t", k=KD),
                                        zt_hi[n % 2][:, :, cols], ALU.subtract).then_inc(zt_ready, 1)

            def update_k(u, g):
                ub, m = u % 2, LEVELS[g - 1]
                n = TC // (2 * m)
                pool.wait_ge(lv_done, L * u + g + 2)
                if g > 1:
                    pool.wait_ge(k_updated, len(LEVELS) * u + g - 1)
                    pool.wait_ge(totalled, len(LEVELS) * u + g - 1)
                else:
                    pool.wait_ge(proj_used, 3 * u + 3)
                right = decay[:, ub, OFF[g - 1]:OFF[g - 1] + TC // m].rearrange("p (n two) -> p n two", two=2)[:, :, 1:2]
                left = k[:, ub, :].rearrange("p (n two m) -> p n two m", two=2, m=m)[:, :, 0, :]
                nc.gpsimd.tensor_tensor(left, left, right.to_broadcast([P, n, m]), ALU.mult).then_inc(k_updated, 1)

            for t in (r[:, 0], r[:, 1]):
                nc.gpsimd.memset(t, 0.0).then_inc(cleared, 1)
            for j in range(TPC):
                z_lo(0, j)
            for t in (mt[:, :, :, :], state[:, :, :, :], carry[:, :, :, :]):
                nc.gpsimd.memset(t, 0.0).then_inc(cleared, 1)
            for u in range(NU):
                for l in range(L):
                    if l >= 2:
                        update_k(u, l - 1)
                    for n, j in tiles_at(T_AT, u, l - 1):
                        if n + 1 < NC:
                            z_lo(n + 1, j)
            for m, (raw, hi, lo) in enumerate(group0):
                pool.wait_ge(group_hi, m + 1)
                nc.gpsimd.tensor_tensor(lo, raw, hi, ALU.subtract).then_inc(group_lo, 1)

        @block.tensor
        def _(pe):
            def half_product(psum, half, lhs_hi, lhs_lo, rhs_hi, rhs_lo, cols, done):
                for kk in range(half * KD // 2, (half + 1) * KD // 2):
                    for n, (lhs, rhs) in enumerate(((lhs_hi, rhs_hi), (lhs_hi, rhs_lo), (lhs_lo, rhs_hi))):
                        last = nc.tensor.matmul(psum, lhs[:, kk, cols], rhs[:, kk, :], start=(kk == 0 and n == 0),
                                                stop=(kk == KD - 1 and n == 2))
                if half:
                    last.then_inc(done, 1)

            def transposes(n, j):
                t = TPC * n + j
                if t >= 2:
                    pe.wait_ge(xn_ready, normed_here(t + 1))
                if j >= 2:
                    pe.wait_ge(z_ready, t - 1)
                elif n >= 2:
                    pe.wait_ge(res_done, TPC * (n - 2) + j + 3)
                elif n:
                    pe.wait_ge(z_ready, j + 3)
                for kk in range(KD):
                    cols = slice(kk * P, (kk + 1) * P)
                    last = nc.tensor.transpose(row[j % 2][:, cols], xn[:, j % 2, cols], ident[:, :])
                last.then_inc(transposed, 1)

            def v_proj(n, j, part):
                t = TPC * n + j
                if part == 0:
                    pe.wait_ge(zt_ready, t + 1)
                    if j >= 2:
                        pe.wait_ge(v_ready, t - 1)
                    elif n:
                        pe.wait_ge(z_ready, TPC * n + j + 3)
                half_product(v_bank(n, j)[:, :], part, zt_hi[n % 2], zt_lo[n % 2], w_hi[WV], w_lo[WV],
                             slice(j * P, (j + 1) * P), v_done)

            def out_proj(n, j, part):
                t = TPC * n + j
                if part == 0:
                    pe.wait_ge(yt_ready, NPAIR * (n + 1))
                    if j >= 2:
                        pe.wait_ge(res_done, t - 1)
                    else:
                        pe.wait_ge(v_ready, TPC * (n + 1) + j + 3)
                    if n == 0:
                        pe.wait_ge(wo_ready, 2)
                half_product(row[j % 2][:, :], part, *y_t[n], w_hi[WO], w_lo[WO],
                             slice(j * P, (j + 1) * P), out_done)

            def out_last(j, pairs):
                if pairs.start == 0:
                    pe.wait_ge(yt_ready, NU - 1)
                    if j < 2:
                        pe.wait_ge(res_done, TPC * (NC - 1) - 1 + j)
                    else:
                        pe.wait_ge(proj_used, 3 * NU)
                else:
                    pe.wait_ge(yt_ready, NU)
                hi, lo = y_t[NC - 1]
                cols = slice(j * P, (j + 1) * P)
                for kk in pairs:
                    for n, (lhs, rhs) in enumerate(((hi, w_hi[WO]), (hi, w_lo[WO]), (lo, w_hi[WO]))):
                        last = nc.tensor.matmul(last_out[j][:, :], lhs[:, kk, cols], rhs[:, kk, :],
                                                start=(kk == 0 and n == 0), stop=(kk == NPAIR - 1 and n == 2))
                if pairs.stop == NPAIR:
                    last.then_inc(out_done, 1)

            def next_transposes(j):
                pe.wait_ge(next_xn_ready, j + 1)
                if j < 2:
                    pe.wait_ge(kept_act, ON_ACT * NU)
                else:
                    pe.wait_ge(next_xt_ready, j - 1)
                for kk in range(KD):
                    cols = slice(kk * P, (kk + 1) * P)
                    last = nc.tensor.transpose(lv[j % 2][:, cols], sh.xn[:, j, cols], ident[:, :])
                last.then_inc(next_transposed, 1)

            def project(u, part):
                n, p, job, third = u // NPAIR, u % NPAIR, part // 3, part % 3
                i3 = 3 * u + job
                if third == 0:
                    pe.wait_ge(zt_ready, TPC * (n + 1))
                    if i3 >= 2:
                        pe.wait_ge(proj_used, i3 - 1)
                w = (WR, WK, WXW)[job]
                cols = slice(p * P, (p + 1) * P)
                passes = [(a, e, kk) for kk in range(KD) for a, e in ((w_hi, zt_hi), (w_hi, zt_lo), (w_lo, zt_hi))]
                for i in range(4 * third, 4 * third + 4):
                    a, e, kk = passes[i]
                    last = nc.tensor.matmul(pj[i3 % 2][:, :], a[w][:, kk, cols], e[n % 2][:, kk, :],
                                            start=(i == 0), stop=(i == len(passes) - 1))
                if third == 2:
                    last.then_inc(proj_done, 1)

            def level(u, l):
                i, ub = L * u + l, u % 2
                if i >= 2:
                    pu, pl = (i - 2) // L, (i - 2) % L
                    if pl < ON_DVE:
                        pe.wait_ge(kept_dve, ON_DVE * pu + pl + 1)
                    else:
                        pe.wait_ge(kept_act, ON_ACT * pu + pl - ON_DVE + 1)
                if l == 0:
                    pe.wait_ge(proj_used, 3 * u + 2)
                if l >= 2:
                    pe.wait_ge(updated, UPD * u + l - 1)
                    if l > 2:
                        pe.wait_ge(k_updated, len(LEVELS) * u + l - 2)
                for q in ((2 * l, 2 * l + 1) if l < 2 else range(Q)):
                    cols = slice(q * P, (q + 1) * P)
                    if l < 2:
                        rhs = r[:, ub, :, cols]
                        out = lv[i % 2][:, (q % 2) * 2 * P:(q % 2 + 1) * 2 * P]
                    else:
                        m = LEVELS[l - 2]
                        rhs = r[:, ub, :, cols].rearrange("p h (n two m) -> p h n two m", two=2, m=m)[:, :, :, 1, :]
                        out = lv[i % 2][:, cols]
                    last = nc.tensor.matmul(out, k[:, ub, cols], rhs, start=True, stop=True)
                last.then_inc(lv_done, 1)

            def k_transposes(u):
                pe.wait_ge(k_updated, len(LEVELS) * (u + 1))
                if u:
                    pe.wait_ge(carried, 2 * u)
                else:
                    pe.wait_ge(v_ready, TPC)
                for q in range(Q):
                    cols = slice(q * P, (q + 1) * P)
                    last = nc.tensor.transpose(ks[:, cols], k[:, u % 2, cols], ident[:, :])
                last.then_inc(kt_done, 1)

            def k_times_v(u):
                n, p = u // NPAIR, u % NPAIR
                pe.wait_ge(ktok_ready, u + 1)
                pe.wait_ge(v_ready, TPC * (n + 1))
                for q in range(Q):
                    cols = slice(q * P, (q + 1) * P)
                    last = nc.tensor.matmul(ks[:, cols], ktok[:, cols], v[n % 2][:, q, p * P:(p + 1) * P],
                                            start=True, stop=True)
                last.then_inc(kv_done, 1)

            def outputs(u):
                n, p, ub = u // NPAIR, u % NPAIR, u % 2
                pe.wait_ge(kept_act, ON_ACT * (u + 1))
                pe.wait_ge(rsum_left, u + 1)
                pe.wait_ge(state_step, 2 * (Q - 1) * (u + 1))
                if u:
                    pe.wait_ge(yt_ready, u)
                for q in range(Q):
                    cols = slice(q * P, (q + 1) * P)
                    s_q = carry[:, n % B, p, :] if q == 0 else state[:, ub, q - 1, :]
                    nc.tensor.matmul(yb[:, cols], s_q, rsum[:, cols], start=True, stop=False, skip_group_check=True)
                    for h in range(2):
                        hp = slice(h * HS, (h + 1) * HS)
                        last = nc.tensor.matmul(yb[hp, cols], v[n % 2][:, q, p * P + h * HS:p * P + (h + 1) * HS],
                                                mt[:, ub, 2 * q + h, :], start=False, stop=True, skip_group_check=True)
                last.then_inc(y_done, 1)

            for j in range(TPC):
                transposes(0, j)
            for i in range(TPC):
                v_proj(0, i // 2, i % 2)
            for part in range(9):
                project(0, part)
            for u in range(NU + 1):
                for l in range(L):
                    if u < NU:
                        level(u, l)
                    if u + 1 < NU:
                        project(u + 1, l)
                    if u and l == 1:
                        k_transposes(u - 1)
                    if u and l == 4:
                        k_times_v(u - 1)
                    if u and l == 7:
                        outputs(u - 1)
                    if (u, l) in V0_AT:
                        v_proj(0, V0_AT[u, l] // 2, V0_AT[u, l] % 2)
                    for n, j in tiles_at(T_AT, u, l):
                        if n + 1 < NC:
                            transposes(n + 1, j)
                    for n, i in tiles_at(V_AT, u, l):
                        if n + 1 < NC:
                            v_proj(n + 1, i // 2, i % 2)
                    for n, i in out_at(u, l):
                        out_proj(n, i // 2, i % 2)
                    if u == NU and l in (2, 3, 5, 6):
                        out_last((2, 3, 5, 6).index(l), range(NPAIR - 1))
                    if u == NU and l in (4, 5, 6, 7):
                        next_transposes(l - 4)
            for j in range(TPC):
                out_last(j, range(NPAIR - 1, NPAIR))

        @block.scalar
        def _(act):
            def z_tile(n, j):
                t = TPC * n + j
                act.wait_ge(transposed, t + 1)
                if t >= 2:
                    act.wait_ge(zt_ready, t - 1)
                if n >= 2:
                    act.wait_ge(v_done, TPC * (n - 1))
                    act.wait_ge(proj_done, 3 * NPAIR * (n - 1))
                for kk in range(KD):
                    cols = slice(kk * P, (kk + 1) * P)
                    last = nc.scalar.activation(z[:, j % 2, cols], row[j % 2][:, cols], ACT.Identity,
                                                bias=beta[:, kk:kk + 1], scale=gamma[:, kk:kk + 1])
                last.then_inc(z_ready, 1)
                act.wait_ge(z_ready, t + 1)
                nc.scalar.activation(zt_hi[n % 2][:, :, j * P:(j + 1) * P],
                                     z[:, j % 2, :].rearrange("p (k t) -> p k t", k=KD), ACT.Copy).then_inc(zhi_ready, 1)

            def v_tile(n, j):
                act.wait_ge(v_done, TPC * n + j + 1)
                if n >= 2:
                    act.wait_ge(y_done, NPAIR * (n - 1))
                nc.scalar.activation(v[n % 2][:, j, :], v_bank(n, j)[:, :], ACT.Copy).then_inc(v_ready, 1)

            def projected(u, job):
                i3, ub, p = 3 * u + job, u % 2, u % NPAIR
                act.wait_ge(proj_done, i3 + 1)
                if job == 0:
                    if u >= 2:
                        act.wait_ge(updated, UPD * (u - 1))
                        act.wait_ge(rsum_left, u - 1)
                    for h in range(2):
                        hp = slice(h * HS, (h + 1) * HS)
                        last = nc.scalar.activation(r[hp, ub, h, :], pj[i3 % 2][hp, :], ACT.Sigmoid)
                elif job == 1:
                    if u >= 2:
                        act.wait_ge(kt_done, u - 1)
                    last = nc.scalar.activation(k[:, ub, :], pj[i3 % 2][:, :], ACT.Copy)
                else:
                    if u >= 2:
                        act.wait_ge(carried, 2 * (u - 1))
                    last = nc.scalar.activation(decay[:, ub, 0:TC], pj[i3 % 2][:, :], ACT.Sigmoid,
                                                bias=neg_bw[:, p:p + 1], scale=-1.0)
                last.then_inc(proj_used, 1)

            def keep_scores(u, l):
                i, m, ub = L * u + l, LEVELS[l - 2], u % 2
                act.wait_ge(lv_done, i + 1)
                if l == ON_DVE:
                    act.wait_ge(kept_dve, ON_DVE * (u + 1))
                nb = P // (2 * m)
                out = mt[:, ub, :, :].rearrange("p g (n two m) -> p g n two m", two=2, m=m)
                src = lv[i % 2][:, :].rearrange("p (g n m) -> p g n m", g=2 * Q, m=m)
                for b in range(nb):
                    rows = slice(2 * m * b, 2 * m * b + m)
                    last = nc.scalar.activation(out[rows, :, b, 1, :], src[rows, :, b, :], ACT.Copy)
                last.then_inc(kept_act, 1)

            def sum_left(u):
                act.wait_ge(updated, UPD * u + UPD - 1)
                if u:
                    act.wait_ge(y_done, u)
                for h in range(2):
                    hp = slice(h * HS, (h + 1) * HS)
                    left = [a.rearrange("p (n two m) -> p n two m", two=2, m=HS)[:, :, 0, :]
                            for a in (rsum[hp, :], r[hp, u % 2, h, :])]
                    last = nc.scalar.activation(left[0], left[1], ACT.Copy)
                last.then_inc(rsum_left, 1)

            def ktok_copy(u):
                act.wait_ge(kt_done, u + 1)
                if u:
                    act.wait_ge(kv_done, u)
                nc.scalar.activation(ktok[:, :], ks[:, :], ACT.Copy).then_inc(ktok_ready, 1)

            def y_hi(u):
                act.wait_ge(y_done, u + 1)
                n = u // NPAIR
                if n == NC - 1:
                    act.wait_ge(proj_done, 3 * NPAIR * n)
                    act.wait_ge(v_done, TPC * n)
                elif n:
                    act.wait_ge(out_done, TPC * n)
                nc.scalar.activation(y_t[n][0][:, u % NPAIR, :], yb[:, :], ACT.Copy).then_inc(yhi_ready, 1)

            def group_high(m):
                act.wait_ge(group_loaded[m], 16)
                act.wait_ge(v_done, NT)
                nc.scalar.activation(group0[m][1], group0[m][0], ACT.Copy).then_inc(group_hi, 1)

            for j in range(TPC):
                z_tile(0, j)
            act.wait_ge(cleared, 2)
            act.wait_ge(negated, 1)
            for j in range(2):
                v_tile(0, j)
            for job in range(3):
                projected(0, job)
            for u in range(NU + 1):
                for l in range(L):
                    if u and l == 8:
                        y_hi(u - 1)
                    if u < NU and l >= ON_DVE:
                        keep_scores(u, l)
                    if u < NU and l == L - 1:
                        sum_left(u)
                    if u + 1 < NU and l % 3 == 2:
                        projected(u + 1, l // 3)
                    if u and l == 2:
                        ktok_copy(u - 1)
                    if V0_AT.get((u, l), 0) % 2:
                        v_tile(0, V0_AT[u, l] // 2)
                    for n, j in tiles_at(T_AT, u, l):
                        if n + 1 < NC:
                            z_tile(n + 1, j)
                    for n, i in tiles_at(V_AT, u, l):
                        if n + 1 < NC and i % 2:
                            v_tile(n + 1, i // 2)
                    if u == NU - 1 and l in (4, 7):
                        group_high(l // 6)
                    if u == NU and 4 <= l < 8:
                        act.wait_ge(proj_done, 3 * NU)
                        transposed_high(nc, act, sh.xt[:, 0], lv[l % 2], l - 4, next_transposed, l - 3).then_inc(next_hi_ready, 1)

        @block.vector
        def _(dve):
            steps = [0]

            def count():
                steps[0] += 1
                return steps[0]

            norm = Norm(nc, dve, ln_step, count, sh)

            def norm_part(n, part):
                if part == 0:
                    dve.wait_ge(x_loaded, 16 * n)
                norm.part(x, part)
                if part == NORM_PARTS - 1:
                    normed(n, 0)
                    normed(n, 1)

            def normed(n, j):
                t = TPC * n + j
                if t >= 2:
                    dve.wait_ge(transposed, t - 1)
                nc.vector.tensor_scalar(xn[:, j % 2, :], x[:, j, :], sh.mv[:, j, 0:1], sh.rstd[:, j:j + 1],
                                        ALU.subtract, ALU.mult).then_inc(xn_ready, 1)

            def update(u, g):
                ub = u % 2
                if g == 0:
                    dve.wait_ge(lv_done, L * u + 2)
                    dve.wait_ge(proj_used, 3 * u + 3)
                    for h in range(2):
                        hp = slice(h * HS, (h + 1) * HS)
                        last = nc.vector.tensor_tensor(r[hp, ub, h, :], r[hp, ub, h, :], decay[hp, ub, 0:TC], ALU.mult)
                    last.then_inc(updated, 1)
                    return
                m = LEVELS[g - 1]
                n = TC // (2 * m)
                dve.wait_ge(lv_done, L * u + g + 2)
                dve.wait_ge(updated, UPD * u + g)
                if g > 1:
                    dve.wait_ge(totalled, len(LEVELS) * u + g - 1)
                if g == UPD - 1 and u:
                    dve.wait_ge(y_done, u)
                total = decay[:, ub, OFF[g - 1]:OFF[g - 1] + TC // m].rearrange("p (n two) -> p n two", two=2)
                for h in range(2):
                    hp = slice(h * HS, (h + 1) * HS)
                    right = r[hp, ub, h, :].rearrange("p (n two m) -> p n two m", two=2, m=m)[:, :, 1, :]
                    new = right
                    if g == UPD - 1:
                        new = rsum[hp, :].rearrange("p (n two m) -> p n two m", two=2, m=m)[:, :, 1, :]
                    last = nc.vector.tensor_tensor(new, right, total[hp, :, 0:1].to_broadcast([HS, n, m]), ALU.mult)
                last.then_inc(updated, 1)
                nc.vector.tensor_tensor(decay[:, ub, OFF[g]:OFF[g] + n], total[:, :, 0], total[:, :, 1],
                                        ALU.mult).then_inc(totalled, 1)

            def keep_scores(u, l):
                i, ub = L * u + l, u % 2
                dve.wait_ge(lv_done, i + 1)
                if l == 0 and u >= 2:
                    dve.wait_ge(y_done, u - 1)
                if l:
                    dve.wait_ge(kept_dve, ON_DVE * u + l)
                if l < 2:
                    out = mt[:, ub, 4 * l:4 * l + 4, :]
                    src = lv[i % 2][:, :].rearrange("p (g t) -> p g t", g=4)
                    mask = masks[:, 0:1, :].to_broadcast([P, 4, P])
                else:
                    m = LEVELS[l - 2]
                    nb = P // (2 * m)
                    out = mt[:, ub, :, :].rearrange("p g (n two m) -> p g n two m", two=2, m=m)[:, :, :, 1, :]
                    src = lv[i % 2][:, :].rearrange("p (g n m) -> p g n m", g=2 * Q, m=m)
                    mask = masks[:, l - 1, :].rearrange("p (n two m) -> p n two m", two=2, m=m)[:, :, 1, :]
                    mask = mask.unsqueeze(1).to_broadcast([P, 2 * Q, nb, m])
                nc.vector.copy_predicated(out, mask, src).then_inc(kept_dve, 1)

            def next_state(u, q):
                n, p, ub = u // NPAIR, u % NPAIR, u % 2
                if q == 0:
                    dve.wait_ge(kv_done, u + 1)
                    dve.wait_ge(totalled, len(LEVELS) * (u + 1))
                    if n >= B:
                        dve.wait_ge(carried, 2 * (u - B * NPAIR + 1))
                else:
                    dve.wait_ge(state_step, 2 * (Q - 1) * u + 2 * q)
                if q == Q - 1:
                    dve.wait_ge(y_done, u + 1)
                for h in range(2):
                    hp = slice(h * HS, (h + 1) * HS)
                    new = state[hp, ub, q, hp] if q < Q - 1 else carry[hp, n % B, p, hp]
                    old = state[hp, ub, q - 1, hp] if q else carry[hp, n % B, p, hp]
                    nc.vector.scalar_tensor_tensor(
                        out=new, in0=old, scalar=decay[hp, ub, OFF[-1] + q:OFF[-1] + q + 1],
                        in1=ks[hp, q * P + h * HS:q * P + (h + 1) * HS],
                        op0=ALU.mult, op1=ALU.add).then_inc(state_step if q < Q - 1 else carried, 1)

            def y_lo(u):
                dve.wait_ge(yhi_ready, u + 1)
                hi, lo = (part[:, u % NPAIR, :] for part in y_t[u // NPAIR])
                nc.vector.tensor_tensor(lo, yb[:, :], hi, ALU.subtract).then_inc(yt_ready, 1)

            def residual(n, j):
                t = TPC * n + j
                dve.wait_ge(out_done, t + 1)
                if n == NC - 1 and j >= 2:
                    dve.wait_ge(last_res_loaded, 16 * 2)
                else:
                    dve.wait_ge(res_loaded[j % 2], 16 * (t // 2 + 1))
                bank = last_out[j] if n == NC - 1 else row[j % 2]
                nc.vector.tensor_tensor(residual_tile(n, j), residual_tile(n, j), bank[:, :],
                                        ALU.add).then_inc(res_done, 1)

            for j in range(2, TPC):
                normed(0, j)
            nc.vector.tensor_scalar(neg_bw[:, :], sh.bw[:, :], -1.0, None, ALU.mult).then_inc(negated, 1)
            for i in range(2):
                half = [part[:, 2 * i:2 * i + 2, :] for part in (w_hi[WO], w_lo[WO])]
                dve.wait_ge(wo_loaded, 16 * (i + 1))
                nc.vector.tensor_copy(half[0], xres[:, :, :]).then_inc(wo_hi_ready, 1)
                dve.wait_ge(wo_hi_ready, i + 1)
                nc.vector.tensor_tensor(half[1], xres[:, :, :], half[0], ALU.subtract).then_inc(wo_ready, 1)
            dve.wait_ge(masks_loaded, 16)
            dve.wait_ge(cleared, 5)
            for u in range(NU + 1):
                for l in range(L):
                    if u and l == 8:
                        y_lo(u - 1)
                    if u < NU:
                        if l:
                            update(u, l - 1)
                        if l < ON_DVE:
                            keep_scores(u, l)
                    if u and l in (5, 6):
                        for q in (range(2), range(2, Q - 1))[l - 5]:
                            next_state(u - 1, q)
                    if u and l == 8 and u < NU:
                        next_state(u - 1, Q - 1)
                    for n, part in tiles_at(NORM_AT, u, l):
                        if n + 1 < NC:
                            norm_part(n + 1, part)
                    if u == NU - 1 and l < Norm.ONCE:
                        if l == 0:
                            dve.wait_ge(next_x_loaded, 16)
                        norm.part(x, l)
                    if u == NU and l < TPC:
                        if l == 0:
                            dve.wait_ge(transposed, NT)
                            dve.wait_ge(zt_ready, NT)
                        norm.normed(x, l).then_inc(next_xn_ready, 1)
                    for n, j in tiles_at(XN_AT, u, l):
                        if n + 1 < NC:
                            normed(n + 1, j)
                    for n, i in out_at(u, l):
                        if i % 2:
                            residual(n, i // 2)
                    if u == NU and 4 <= l < 8:
                        transposed_low(nc, dve, sh.xt[:, 0], lv[l % 2], l - 4, next_hi_ready, l - 3).then_inc(next_xt_ready, 1)
            for j in range(TPC):
                residual(NC - 1, j)


def build(nc, x, w1g, w3g, w2t, wxt, ww, wk, wv, wr, wo, bw, gamma, beta, had, ident, masks, out):
    def scratch(name, shape, dt=F32):
        return nc.dram_tensor(name, shape, dt, kind="Internal").ap()
    w2p = scratch("w2p", [NG, P, HT, D])
    wxw = scratch("wxw", [P, KD, D])
    x1 = scratch("x1", [B * T, D])
    x2 = scratch("x2", [B * T, D])
    wr_v, wk_v, wv_v, wo_v = (w.rearrange("(k p) d -> p k d", p=P) for w in (wr, wk, wv, wo))
    with ExitStack() as ctx:
        sh = Shared(nc, ctx)
        prepare_weights(nc, sh, x, w1g, w3g, w2t, wxt, ww, had, ident, gamma, beta, bw, w2p, wxw)
        feed_forward(nc, sh, "ffn1", x, x1, w1g, w3g, w2p, None, sh.stored[0], (wr_v, wk_v, wxw, wv_v))
        mixing(nc, sh, x1, x2, w1g, w3g, wo_v, masks, (sh.stored[0], 16 * NT), sh.stored[1])
        feed_forward(nc, sh, "ffn2", x2, out, w1g, w3g, w2p, (sh.stored[1], 16 * TPC), None, None)


def kernel(**inputs):
    import numpy as np
    import concourse.bacc as bacc
    from concourse.bass_utils import run_bass_kernel_spmd

    arr = {n: np.asarray(a) for n, a in inputs.items()}
    up = lambda w: np.ascontiguousarray(w.reshape(NG, GH, KD, P).transpose(0, 3, 2, 1))
    cols = lambda v: np.ascontiguousarray(v.reshape(KD, P).T)
    i = np.arange(P)
    bits = i[:, None] & i[None, :]
    odd = sum((bits >> n) & 1 for n in range(7)) & 1
    s, t = i[:, None], i[None, :]
    masks = [s == t] + [(s // (2 * m) == t // (2 * m)) & (s % (2 * m) < m) & (t % (2 * m) >= m) for m in LEVELS[:4]]
    data = {
        "x": arr["L0_attn_x"].reshape(B * T, D),
        "w1g": up(arr["L0_ffn_W1"]),
        "w3g": up(arr["L0_ffn_W3"]),
        "w2t": np.ascontiguousarray(arr["L0_ffn_W2"].T),
        "wxt": np.ascontiguousarray(arr["L0_attn_Wx"].T),
        "ww": arr["L0_attn_Ww"],
        "wk": arr["L0_attn_Wk"],
        "wv": arr["L0_attn_Wv"],
        "wr": arr["L0_attn_Wr"],
        "wo": arr["L0_attn_Wout"],
        "bw": cols(arr["L0_attn_bw"]),
        "gamma": cols(arr["L0_attn_gamma"]),
        "beta": cols(arr["L0_attn_beta"]),
        "had": np.stack([np.where(odd == 1, -1, 1), np.where(odd == 1, 1, -1)], 1).astype(np.float32),
        "ident": np.eye(P, dtype=np.float32),
        "masks": np.ascontiguousarray(np.stack(masks, 1).astype(np.int32)),
    }
    nc = bacc.Bacc("TRN2", target_bir_lowering=False, num_devices=1, dynamic_dma_scratch_size=1024)
    aps = {n: nc.dram_tensor(f"in_{n}", a.shape, mybir.dt.from_np(a.dtype), kind="ExternalInput").ap()
           for n, a in data.items()}
    out = nc.dram_tensor("out_x", (B * T, D), F32, kind="ExternalOutput").ap()
    build(nc, **aps, out=out)
    res = run_bass_kernel_spmd(nc, [{f"in_{n}": a for n, a in data.items()}], core_ids=[0])
    return res.results[0]["out_x"].reshape(B, T, D)
```
